# Optimizing a Trainium2 kernel written in Bass

```python
import numpy as np
import jax
import jax.numpy as jnp

def _softmax(x, axis=-1):
    return jax.nn.softmax(x, axis=axis)

def _gelu(x):
    return jax.nn.gelu(x, approximate=True)

def _silu(x):
    return jax.nn.silu(x)

def _sigmoid(x):
    return jax.nn.sigmoid(x)

def _layernorm(x, axis=-1, eps=1e-05):
    m = jnp.mean(x, axis=axis, keepdims=True)
    v = jnp.var(x, axis=axis, keepdims=True)
    return (x - m) / jnp.sqrt(v + eps)

def _scatter_add(tgt, idx, src, axis=0):
    return tgt.at[idx].add(src)

def _segment_sum(src, seg, n):
    return jax.ops.segment_sum(src, seg, n)
kernel_name = 'mk_rec_standalone_d1_rec_r8_0d7084'

def setup_inputs(seed: int=0):
    np.random.seed(seed)
    _w = jnp.asarray

    def _rec_inputs():
        import jax
        import jax.numpy as jnp
        _rk = jax.random.key(seed)
        r_conts = jax.random.uniform(jax.random.fold_in(_rk, 1), (2048, 13), jnp.float32, 0.0, 1)
        r_cates = jnp.stack([jax.random.randint(jax.random.fold_in(jax.random.fold_in(_rk, 2), 0), (2048,), 2, 12500, jnp.int32), jax.random.randint(jax.random.fold_in(jax.random.fold_in(_rk, 2), 1), (2048,), 1, 99999, jnp.int32), jax.random.randint(jax.random.fold_in(jax.random.fold_in(_rk, 2), 2), (2048,), 0, 12500, jnp.int32), jax.random.randint(jax.random.fold_in(jax.random.fold_in(_rk, 2), 3), (2048,), 5, 12500, jnp.int32), jax.random.randint(jax.random.fold_in(jax.random.fold_in(_rk, 2), 4), (2048,), 20, 99993, jnp.int32), jax.random.randint(jax.random.fold_in(jax.random.fold_in(_rk, 2), 5), (2048,), 0, 99993, jnp.int32), jax.random.randint(jax.random.fold_in(jax.random.fold_in(_rk, 2), 6), (2048,), 2, 99999, jnp.int32), jax.random.randint(jax.random.fold_in(jax.random.fold_in(_rk, 2), 7), (2048,), 2, 99995, jnp.int32), jax.random.randint(jax.random.fold_in(jax.random.fold_in(_rk, 2), 8), (2048,), 0, 99999, jnp.int32), jax.random.randint(jax.random.fold_in(jax.random.fold_in(_rk, 2), 9), (2048,), 2, 99986, jnp.int32), jax.random.randint(jax.random.fold_in(jax.random.fold_in(_rk, 2), 10), (2048,), 4, 99999, jnp.int32), jax.random.randint(jax.random.fold_in(jax.random.fold_in(_rk, 2), 11), (2048,), 15, 99999, jnp.int32), jax.random.randint(jax.random.fold_in(jax.random.fold_in(_rk, 2), 12), (2048,), 0, 99989, jnp.int32), jax.random.randint(jax.random.fold_in(jax.random.fold_in(_rk, 2), 13), (2048,), 5, 99990, jnp.int32), jax.random.randint(jax.random.fold_in(jax.random.fold_in(_rk, 2), 14), (2048,), 2, 99996, jnp.int32), jax.random.randint(jax.random.fold_in(jax.random.fold_in(_rk, 2), 15), (2048,), 3, 99994, jnp.int32), jax.random.randint(jax.random.fold_in(jax.random.fold_in(_rk, 2), 16), (2048,), 0, 99998, jnp.int32), jax.random.randint(jax.random.fold_in(jax.random.fold_in(_rk, 2), 17), (2048,), 13, 99998, jnp.int32), jax.random.randint(jax.random.fold_in(jax.random.fold_in(_rk, 2), 18), (2048,), 10, 12498, jnp.int32), jax.random.randint(jax.random.fold_in(jax.random.fold_in(_rk, 2), 19), (2048,), 0, 99999, jnp.int32), jax.random.randint(jax.random.fold_in(jax.random.fold_in(_rk, 2), 20), (2048,), 0, 99995, jnp.int32), jax.random.randint(jax.random.fold_in(jax.random.fold_in(_rk, 2), 21), (2048,), 1, 99998, jnp.int32), jax.random.randint(jax.random.fold_in(jax.random.fold_in(_rk, 2), 22), (2048,), 1, 99997, jnp.int32), jax.random.randint(jax.random.fold_in(jax.random.fold_in(_rk, 2), 23), (2048,), 2, 99989, jnp.int32), jax.random.randint(jax.random.fold_in(jax.random.fold_in(_rk, 2), 24), (2048,), 6, 12500, jnp.int32), jax.random.randint(jax.random.fold_in(jax.random.fold_in(_rk, 2), 25), (2048,), 2, 99995, jnp.int32)], axis=1)
        return (r_conts, r_cates)
    r_conts, r_cates = _rec_inputs()

    def _L0_rec_setup():
        import jax, jax.numpy as jnp
        import numpy as np
        CONT_FIELD = 13
        CATE_FIELD = 26
        VOCAB = 12500
        EMB_DIM = 64
        HIDDEN = [1024, 1024]
        B = 2048
        N_FIELDS = CONT_FIELD + CATE_FIELD
        COMB = N_FIELDS * (N_FIELDS - 1) // 2
        FIRST = EMB_DIM * N_FIELDS + COMB
        _ROWS, _COLS = np.triu_indices(N_FIELDS, k=1)
        ROWS = jnp.asarray(_ROWS)
        COLS = jnp.asarray(_COLS)

        def _layernorm(x, g, b, eps=1e-05):
            mu = jnp.mean(x, axis=-1, keepdims=True)
            var = jnp.mean((x - mu) ** 2, axis=-1, keepdims=True)
            return (x - mu) * jax.lax.rsqrt(var + eps) * g + b
        key = jax.random.key(seed)
        ks = jax.random.split(key, 12)
        a = np.square(3.0 / (CATE_FIELD * EMB_DIM))
        inp = {'conts': jax.random.uniform(ks[0], (B, CONT_FIELD), dtype=jnp.float32), 'cates': jax.random.randint(ks[1], (B, CATE_FIELD), 0, VOCAB), 'combs': jax.random.normal(ks[2], (B, COMB), dtype=jnp.float32), 'emb_table': jax.random.uniform(ks[3], (VOCAB, EMB_DIM), minval=-a, maxval=a, dtype=jnp.float32), 'W1': jax.random.normal(ks[4], (FIRST, HIDDEN[0]), dtype=jnp.float32) * (6.0 / (FIRST + HIDDEN[0])) ** 0.5, 'b1': jnp.zeros((HIDDEN[0],), jnp.float32), 'ln1_g': jnp.ones((HIDDEN[0],), jnp.float32), 'ln1_b': jnp.zeros((HIDDEN[0],), jnp.float32), 'W2': jax.random.normal(ks[5], (HIDDEN[0], HIDDEN[1]), dtype=jnp.float32) * (6.0 / (HIDDEN[0] + HIDDEN[1])) ** 0.5, 'b2': jnp.zeros((HIDDEN[1],), jnp.float32), 'ln2_g': jnp.ones((HIDDEN[1],), jnp.float32), 'ln2_b': jnp.zeros((HIDDEN[1],), jnp.float32), 'Wout': jax.random.normal(ks[6], (HIDDEN[1], 1), dtype=jnp.float32) * (6.0 / (HIDDEN[1] + 1)) ** 0.5, 'bout': jnp.zeros((1,), jnp.float32)}
        return inp
    _L0_rec_all = _L0_rec_setup()
    _L0_rec_in = {k: v for k, v in _L0_rec_all.items() if k in ('combs', 'emb_table', 'W1', 'b1', 'ln1_g', 'ln1_b', 'W2', 'b2', 'ln2_g', 'ln2_b', 'Wout', 'bout')}
    del _L0_rec_all
    return {'r_conts': r_conts, 'r_cates': r_cates, 'L0_rec_combs': _L0_rec_in['combs'], 'L0_rec_emb_table': _L0_rec_in['emb_table'], 'L0_rec_W1': _L0_rec_in['W1'], 'L0_rec_b1': _L0_rec_in['b1'], 'L0_rec_ln1_g': _L0_rec_in['ln1_g'], 'L0_rec_ln1_b': _L0_rec_in['ln1_b'], 'L0_rec_W2': _L0_rec_in['W2'], 'L0_rec_b2': _L0_rec_in['b2'], 'L0_rec_ln2_g': _L0_rec_in['ln2_g'], 'L0_rec_ln2_b': _L0_rec_in['ln2_b'], 'L0_rec_Wout': _L0_rec_in['Wout'], 'L0_rec_bout': _L0_rec_in['bout']}

def reference(r_conts, r_cates, L0_rec_combs, L0_rec_emb_table, L0_rec_W1, L0_rec_b1, L0_rec_ln1_g, L0_rec_ln1_b, L0_rec_W2, L0_rec_b2, L0_rec_ln2_g, L0_rec_ln2_b, L0_rec_Wout, L0_rec_bout):
    import jax
    import jax.numpy as jnp

    def _L0_rec_ref(conts, cates, combs, emb_table, W1, b1, ln1_g, ln1_b, W2, b2, ln2_g, ln2_b, Wout, bout):
        import jax, jax.numpy as jnp
        import numpy as np
        CONT_FIELD = 13
        CATE_FIELD = 26
        VOCAB = 12500
        EMB_DIM = 64
        HIDDEN = [1024, 1024]
        B = 2048
        N_FIELDS = CONT_FIELD + CATE_FIELD
        COMB = N_FIELDS * (N_FIELDS - 1) // 2
        FIRST = EMB_DIM * N_FIELDS + COMB
        _ROWS, _COLS = np.triu_indices(N_FIELDS, k=1)
        ROWS = jnp.asarray(_ROWS)
        COLS = jnp.asarray(_COLS)

        def _layernorm(x, g, b, eps=1e-05):
            mu = jnp.mean(x, axis=-1, keepdims=True)
            var = jnp.mean((x - mu) ** 2, axis=-1, keepdims=True)
            return (x - mu) * jax.lax.rsqrt(var + eps) * g + b
        cont_emb = emb_table[:CONT_FIELD][None, :, :] * conts[:, :, None]
        cate_emb = emb_table[cates]
        cc = jnp.concatenate([cont_emb, cate_emb], axis=1)
        gram = jnp.einsum('bfd,bgd->bfg', cc, cc)
        pairs = gram[:, ROWS, COLS]
        X = jnp.concatenate([cont_emb.reshape(cc.shape[0], -1), cate_emb.reshape(cc.shape[0], -1), pairs], axis=1)
        X = jax.nn.relu(_layernorm(X @ W1 + b1, ln1_g, ln1_b))
        X = jax.nn.relu(_layernorm(X @ W2 + b2, ln2_g, ln2_b))
        logit = jax.nn.sigmoid(X @ Wout + bout)
        return logit
    y = _L0_rec_ref(r_conts, r_cates, L0_rec_combs, L0_rec_emb_table, L0_rec_W1, L0_rec_b1, L0_rec_ln1_g, L0_rec_ln1_b, L0_rec_W2, L0_rec_b2, L0_rec_ln2_g, L0_rec_ln2_b, L0_rec_Wout, L0_rec_bout)
    return y

_drawn_inputs = setup_inputs


def setup_inputs(seed=0):
    import zlib

    import numpy as np

    out = dict(_drawn_inputs(seed))
    spreads = {'L0_rec_b1': (0.0, 0.1),
     'L0_rec_ln1_g': (1.0, 0.6),
     'L0_rec_ln1_b': (0.0, 2.0),
     'L0_rec_b2': (0.0, 0.589),
     'L0_rec_ln2_g': (1.0, 0.2),
     'L0_rec_ln2_b': (0.0, 0.35)}
    factors = {'r_conts': 64.0, 'L0_rec_emb_table': 64.0, 'L0_rec_W1': 64.0}
    for name, (base, spread) in spreads.items():
        noise = np.random.default_rng([zlib.crc32(name.encode()), seed]).standard_normal(out[name].shape)
        drawn = base * np.exp(spread * noise) if base else spread * noise
        out[name] = jnp.asarray(drawn.astype(out[name].dtype))
    for name, factor in factors.items():
        out[name] = (out[name] * factor).astype(out[name].dtype)
    return out
```

```python
from contextlib import ExitStack

import numpy as np
import concourse.bass as bass
from concourse import mybir

F32 = mybir.dt.float32
F32R = mybir.dt.float32r
I32 = mybir.dt.int32
U32 = mybir.dt.uint32
ALU = mybir.AluOpType
ACT = mybir.ActivationFunctionType

P = 128
BATCH = 2048
TILES = BATCH // P
CONT = 13
CATE = 26
FIELDS = CONT + CATE
DIM = 64
VOCAB = 12500
HID = 1024
HALF = HID // 2
EPS = 1e-5
PAIR_ROW0 = FIELDS * DIM
EK = CATE * DIM // P
CC = CONT * CATE
NN = CONT * (CONT - 1) // 2
PACKED = CC + NN + CONT + 1
FT = 3
PART = PACKED - FT * P
V_AT = PART - 1 - CONT
DIAG = 25
DIAGS = 13
SHARED = PART + 3 * DIAG
WHOLE = 5 * DIAG
FK = 6
KT = EK + FK
K2 = HID // P
GROUPS = ((0, 4), (4, 7), (7, 10), (10, 13))
NG = len(GROUPS)
QUAD = 32
FILLS = 8
G_ROW = CATE * QUAD
G_PITCH = (CATE + 1) * G_ROW
STAGES = 3
V_TILES = (CONT + 1) // 2


def field_of(f):
    return 2 * f if f < EK else 2 * (f - EK) + 1


def pair_row(i, j):
    i, j = min(i, j), max(i, j)
    return PAIR_ROW0 + i * FIELDS - i * (i + 1) // 2 + (j - i - 1)


def feature_rows():
    rows = np.zeros((P, FK), np.int32)
    packed = [pair_row(i, CONT + g) for i in range(CONT) for g in range(CATE)]
    packed += [pair_row(i, (i + k) % CONT) for k in range(1, CONT // 2 + 1) for i in range(CONT)]
    packed += [0] * (CONT + 1)
    for c, r in enumerate(packed):
        rows[c % P, c // P] = r
    for k in range(1, DIAGS + 1):
        for f in range(DIAG):
            a, b = (f, f + k) if f + k < CATE else (f + 1, f + k - CATE)
            slot, at = diag_place(k)
            rows[at + f, slot] = pair_row(CONT + field_of(a), CONT + field_of(b))
    return rows


def diag_place(k):
    if k <= 5:
        return 4, DIAG * (k - 1)
    if k <= 10:
        return 5, DIAG * (k - 6)
    return 3, PART + DIAG * (k - 11)


def build(nc, conts, cates, emb, W1, b1, g1, be1, W2, b2, g2, be2, Wout, bout, rows, out):
    h1_dram = nc.dram_tensor("h1_scratch", (P, TILES, HID), F32, kind="Internal").ap()
    dots_dram = nc.dram_tensor("dots_scratch", (4 * G_PITCH,), F32, kind="Internal").ap()
    dots_in = dots_dram.rearrange("(s p n) -> s p n", s=4, p=CATE + 1)
    dots_by_s = dots_dram.rearrange("(s x) -> s x", s=4)

    with ExitStack() as both, ExitStack() as one:
        def sb(name, shape, dt=F32, ctx=both):
            return ctx.enter_context(nc.sbuf_tensor(name, shape, dt))

        def sem(name):
            return both.enter_context(nc.semaphore(name))

        stage = sb("stage", [P, STAGES, HID])
        ident = sb("ident", [P, P])
        bn = sb("bn", [P, 2, 6])
        mv = sb("mv", [P, 2])
        st = sb("st", [P, 8])
        logit = sb("logit", [P, TILES])
        prob = sb("prob", [P, TILES])
        bout_bc = sb("bout_bc", [P, 1])
        g1_col = sb("g1_col", [P, K2])
        be1_col = sb("be1_col", [P, K2])

        two = ExitStack()
        w2_hi = sb("w2_hi", [P, K2, HID], F32R, two)
        w2_lo = sb("w2_lo", [P, K2, HID], F32R, two)
        h1 = sb("h1", [P, 2, HID], F32, two)
        y = sb("y", [P, K2, P], F32, two)
        y_hi = sb("y_hi", [P, 2, K2, P], F32R, two)
        y_lo = sb("y_lo", [P, 2, K2, P], F32R, two)
        h2 = sb("h2", [P, HID], F32, two)
        n2 = sb("n2", [P, 2, HID], F32, two)
        a2 = sb("a2", [P, 2, HID], F32, two)
        r2 = sb("r2", [P, HID], F32, two)
        b2_bc = sb("b2_bc", [P, HID], F32, two)
        g2_bc = sb("g2_bc", [P, HID], F32, two)
        be2_bc = sb("be2_bc", [P, HID], F32, two)
        wout_bc = sb("wout_bc", [P, HID], F32, two)
        two.close()

        w1_hi = sb("w1_hi", [P, KT, HID], F32R, one)
        w1_lo = sb("w1_lo", [P, KT, HID], F32R, one)
        x_hi = sb("x_hi", [P, 32, P], F32R, one)
        x_lo = sb("x_lo", [P, 32, P], F32R, one)
        xb = sb("xb", [P, CATE * DIM], F32, one)
        dots = sb("dots", [4 * CATE, 4, CATE, QUAD], F32, one)
        feats = sb("feats", [P, PACKED], F32, one)
        late = sb("late", [P, 3, P], F32, one)
        c2 = sb("c2", [P, 2, 2 * CONT], F32, one)
        cc_dots = sb("cc_dots", [P, NN], F32, one)
        cates_sb = sb("cates_sb", [P, 2, CATE], I32, one)
        shift = sb("shift", [P, CATE], F32, one)
        cates_f = sb("cates_f", [P, CATE], F32, one)
        idx = sb("idx", [P, 2, CATE], U32, one)
        rows_sb = sb("rows_sb", [P, FK], U32, one)
        eT = sb("eT", [P, CONT], F32, one)
        ebd = sb("ebd", [P, 2 * CONT], F32, one)
        ebd_hi = sb("ebd_hi", [P, 2 * CONT], F32R, one)
        ebd_lo = sb("ebd_lo", [P, 2 * CONT], F32R, one)
        ee = late[0:DIM, 0, 0:NN]
        ones = late[0:DIM, 1, :]
        e13 = late[0:CONT, 2, :].rearrange("p (a d) -> p a d", a=2)
        vbd = sb("vbd", [P, V_TILES, CONT], F32, one)

        def pb(name):
            return both.enter_context(nc.psum_tensor(name, [P, 2, HALF], F32))

        acc = [pb("acc0"), pb("acc1")]
        tr = pb("tr")
        gr = pb("gr")

        cates_in = [sem("cates_in0"), sem("cates_in1")]
        conts_in = [sem("conts_in0"), sem("conts_in1")]
        e13_in = sem("e13_in")
        rows_in = sem("rows_in")
        idx_step = sem("idx_step")
        ident_ready = sem("ident_ready")
        stage_in = [sem(f"stage_in{i}") for i in range(STAGES)]
        rows_staged = [sem(f"rows_staged{s}") for s in range(FK)]
        b1_in = sem("b1_in")
        v_in = sem("v_in")
        stage_hi = sem("stage_hi")
        stage_free = sem("stage_free")
        v_free = sem("v_free")
        v_ready = sem("v_ready")
        eT_ready = sem("eT_ready")
        setup = sem("setup")
        vbd_ready = sem("vbd_ready")
        s_ready = sem("s_ready")
        setup_done = sem("setup_done")
        gathered = [sem(f"gathered{g}") for g in range(NG)]
        trans_ready = sem("trans_ready")
        ts_hi = sem("ts_hi")
        ts_lo = sem("ts_lo")
        c_ready = sem("c_ready")
        cc_done = sem("cc_done")
        feat_done = sem("feat_done")
        f_trans = sem("f_trans")
        f_hi = sem("f_hi")
        f_lo = sem("f_lo")
        gram_ready = sem("gram_ready")
        gram_act = sem("gram_act")
        gram_dve = sem("gram_dve")
        dots_out = sem("dots_out")
        late_in = sem("late_in")
        late_hi = sem("late_hi")
        late_done = sem("late_done")
        acc_ready = sem("acc_ready")
        w1_free = sem("w1_free")
        ln = sem("ln")
        sqrt_done = sem("sqrt_done")
        norm_act = sem("norm_act")
        norm_dve = sem("norm_dve")
        h1_out = [sem("h1_out0"), sem("h1_out1")]
        w2_in = [sem(f"w2_in{i}") for i in range(STAGES)]
        w2_hi_done = sem("w2_hi_done")
        w2_done = sem("w2_done")
        g1_in = sem("g1_in")
        par_in = sem("par_in")
        h1_in = [sem("h1_in0"), sem("h1_in1")]
        t2_ready = sem("t2_ready")
        y_ready = sem("y_ready")
        y_hi_done = sem("y_hi_done")
        y_split = sem("y_split")
        acc2_ready = sem("acc2_ready")
        h2_done = sem("h2_done")
        n2_ready = sem("n2_ready")
        a2_mul = sem("a2_mul")
        a2_ready = sem("a2_ready")
        logit_done = sem("logit_done")
        prob_done = sem("prob_done")
        out_done = sem("out_done")
        passed = sem("passed")

        LN_STEPS = 8

        def at(x):
            return slice(x, x + 1) if isinstance(x, int) else bass.ds(x, 1)

        block = both.enter_context(nc.Block())

        def stands_alone(eng):
            eng.sem_inc(passed, 1)

        def stage_wait(eng, n):
            m = n - STAGES
            if m >= 0:
                if m < V_TILES:
                    eng.wait_ge(v_free, m + 1)
                else:
                    eng.wait_ge(stage_free, m - V_TILES + 1)

        def staged(n):
            s = n - V_TILES - EK
            return (stage_in[n % STAGES], 16 * (n // STAGES + 1)) if s < 0 else (rows_staged[s], 16)

        @block.sync
        def _(sp):
            conts_v = conts.rearrange("(p x) f -> p x f", x=TILES)

            def load_conts(x, par):
                if not isinstance(x, int) or x >= 2:
                    sp.wait_ge(feat_done, x - 1)
                    stands_alone(sp)
                for r in range(2):
                    sp.dma_start(c2[:, par, r * CONT:(r + 1) * CONT],
                                 conts_v[:, at(x), :].rearrange("p o f -> p (o f)")).then_inc(conts_in[par], 16)

            sp.dma_start(e13[:, 0, :], emb[0:CONT, :]).then_inc(e13_in, 16)
            sp.dma_start(e13[:, 1, :], emb[0:CONT, :]).then_inc(e13_in, 16)
            load_conts(0, 0)
            load_conts(1, 1)
            for n in range(V_TILES + EK):
                stage_wait(sp, n)
                buf = stage[:, n % STAGES, :]
                if n < V_TILES:
                    m = min(P, CONT * DIM - n * P)
                    sp.dma_start(buf[0:m, :], W1[n * P:n * P + m, :]).then_inc(stage_in[n % STAGES], 16)
                else:
                    r = CONT * DIM + (n - V_TILES) * P
                    sp.dma_start(buf, W1[r:r + P, :]).then_inc(stage_in[n % STAGES], 16)

            def dots_round_trip(x):
                sp.wait_ge(gram_act, 4 * x + 4)
                sp.wait_ge(gram_dve, 4 * x + 4)
                stands_alone(sp)
                sp.wait_ge(late_in, 16 * DIAGS * x)
                stands_alone(sp)
                for s in range(4):
                    sp.dma_start(dots_in[s, 0:CATE, :],
                                 dots[s::4, s, :, :].rearrange("p g j -> p (g j)")).then_inc(dots_out, 16)
                sp.wait_ge(dots_out, 64 * x + 64)
                sp.wait_ge(late_done, x)
                for k in range(1, DIAGS + 1):
                    slot, row = diag_place(k)
                    step = G_ROW + QUAD
                    src = dots_by_s[:, k * QUAD:k * QUAD + DIAG * step]
                    src = src.rearrange("s (f n) -> f s n", n=step)[:, :, 0:QUAD]
                    dst = late[row:row + DIAG, slot - FT, :].rearrange("p (s j) -> p s j", s=4)
                    sp.dma_start(dst, src).then_inc(late_in, 16)

            def h1_store(x, par):
                sp.wait_ge(norm_act, x + 1)
                sp.wait_ge(norm_dve, x + 1)
                stands_alone(sp)
                sp.dma_start(h1_dram[:, at(x), :].rearrange("p o n -> p (o n)"),
                             stage[:, par, :]).then_inc(h1_out[par], 16)

            dots_round_trip(0)
            n = V_TILES + EK + FT
            sp.wait_ge(*staged(n))
            sp.dma_start(stage[PART - 1:PART, n % STAGES, :], b1.unsqueeze(0)).then_inc(b1_in, 16)
            dots_round_trip(1)

            def iteration(x, par):
                h1_store(x - 1, 1 - par)
                load_conts(x + 1, 1 - par)
                dots_round_trip(x + 1)

            iteration(1, 1)
            iteration(2, 0)
            with sp.Fori(0, (TILES - 4) // 2) as i:
                for u in range(2):
                    iteration(2 * i + (3 + u), 1 - u)
            h1_store(TILES - 2, 0)

            def load_w2(k):
                b = (k + 2) % STAGES
                if k >= STAGES:
                    sp.wait_ge(w2_done, k - STAGES + 1)
                sp.dma_start(stage[:, b, :], W2[k * P:k * P + P, :]).then_inc(w2_in[b], 16)

            def load_h1(x, par):
                if not isinstance(x, int) or x >= 2:
                    sp.wait_ge(t2_ready, x - 1)
                    stands_alone(sp)
                sp.dma_start(h1[:, par, :], h1_dram[:, at(x), :].rearrange("p o n -> p (o n)")).then_inc(h1_in[par], 16)

            load_w2(0)
            sp.wait_ge(h1_out[0], 16 * (TILES // 2))
            load_w2(1)
            sp.wait_ge(acc_ready, TILES)
            load_h1(0, 0)
            h1_store(TILES - 1, 1)
            sp.wait_ge(h1_out[1], 16 * (TILES // 2))
            load_h1(1, 1)
            for k in range(2, K2):
                load_w2(k)
            sp.dma_start(b2_bc[:, :], b2.unsqueeze(0).to_broadcast([P, HID])).then_inc(par_in, 16)
            sp.dma_start(g2_bc[:, :], g2.unsqueeze(0).to_broadcast([P, HID])).then_inc(par_in, 16)
            sp.dma_start(be2_bc[:, :], be2.unsqueeze(0).to_broadcast([P, HID])).then_inc(par_in, 16)
            sp.dma_start(wout_bc[:, :], Wout.rearrange("n o -> o n").to_broadcast([P, HID])).then_inc(par_in, 16)
            with sp.Fori(0, (TILES - 2) // 2) as i:
                for u in range(2):
                    load_h1(2 * i + (2 + u), u)
            sp.wait_ge(prob_done, 1)
            sp.dma_start(out.rearrange("(p x) o -> p (x o)", x=TILES), prob[:, :]).then_inc(out_done, 16)
            sp.wait_ge(out_done, 16)

        @block.gpsimd
        def _(pool):
            nc.gpsimd.memset(ident[:, :], 0.0).then_inc(ident_ready, 1)
            pool.wait_ge(ident_ready, 1)
            nc.gpsimd.affine_select(out=ident[:, :], in_=ident[:, :], compare_op=ALU.not_equal, fill=1.0,
                                    base=0, pattern=[[-1, P]], channel_multiplier=1).then_inc(ident_ready, 1)
            cates_v = cates.rearrange("(p x) f -> p x f", x=TILES)

            def load_cates(x, par):
                pool.dma_start(cates_sb[:, par, :],
                               cates_v[:, at(x), :].rearrange("p o f -> p (o f)")).then_inc(cates_in[par], 16)

            def gather(x, par, first=False, last=False):
                if not isinstance(x, int) or x >= 2:
                    for g in range(NG):
                        n = 16 * 2 * (GROUPS[g][1] - GROUPS[g][0])
                        pool.wait_ge(gathered[g], (x - 1) * n)
                pool.wait_ge(cates_in[par], 8 * x + 16 - 8 * par)
                stands_alone(pool)
                nc.gpsimd.tensor_copy(cates_f[:, :], cates_sb[:, par, :]).then_inc(idx_step, 1)
                pool.wait_ge(idx_step, 4 * x + 1)
                stands_alone(pool)
                nc.gpsimd.tensor_scalar(shift[:, :], cates_f[:, :], 0.0, float(VOCAB),
                                        ALU.is_lt, ALU.mult).then_inc(idx_step, 1)
                pool.wait_ge(idx_step, 4 * x + 2)
                stands_alone(pool)
                nc.gpsimd.tensor_tensor(cates_f[:, :], cates_f[:, :], shift[:, :], ALU.add).then_inc(idx_step, 1)
                pool.wait_ge(idx_step, 4 * x + 3)
                stands_alone(pool)
                nc.gpsimd.tensor_scalar(idx[:, par, :].bitcast(I32), cates_f[:, :], 0.0, float(VOCAB - 1),
                                        ALU.max, ALU.min).then_inc(idx_step, 1)
                pool.wait_ge(idx_step, 4 * x + 4)
                stands_alone(pool)
                if not last:
                    load_cates(x + 2, par)
                for g, (a, b) in enumerate(GROUPS):
                    if not first:
                        pool.wait_ge(trans_ready, NG * (x - 1) + g + 1)
                        stands_alone(pool)
                    for f in range(2 * a, 2 * b):
                        nc.gpsimd.indirect_dma_start(
                            out=xb[:, f * DIM:(f + 1) * DIM], out_offset=None, in_=emb,
                            in_offset=bass.IndirectOffsetOnAxis(ap=idx[:, par, f:f + 1], axis=0),
                        ).then_inc(gathered[g], 16)

            load_cates(0, 0)
            load_cates(1, 1)
            gather(0, 0, first=True)
            gather(1, 1)
            pool.wait_ge(rows_in, 16)
            for s in range(FK):
                n = V_TILES + EK + s
                m = P if s < FT else SHARED if s == FT else WHOLE
                stage_wait(pool, n)
                nc.gpsimd.indirect_dma_start(
                    out=stage[0:m, n % STAGES, :], out_offset=None, in_=W1,
                    in_offset=bass.IndirectOffsetOnAxis(ap=rows_sb[0:m, s:s + 1], axis=0),
                ).then_inc(rows_staged[s], 16)
            with pool.Fori(0, (TILES - 4) // 2) as i:
                for u in range(2):
                    gather(2 * i + (2 + u), u)
            gather(TILES - 2, 0, last=True)
            gather(TILES - 1, 1, last=True)

            def affine2(x, par):
                pool.wait_ge(n2_ready, x + 1)
                if not isinstance(x, int) or x >= 2:
                    pool.wait_ge(logit_done, x - 1)
                nc.gpsimd.tensor_tensor(a2[:, par, :], n2[:, par, :], g2_bc[:, :], ALU.mult).then_inc(a2_mul, 1)
                pool.wait_ge(a2_mul, x + 1)
                nc.gpsimd.tensor_tensor(a2[:, par, :], a2[:, par, :], be2_bc[:, :], ALU.add).then_inc(a2_ready, 1)

            pool.wait_ge(par_in, 16 * 4)
            for x in range(2):
                affine2(x, x)
            with pool.Fori(0, (TILES - 2) // 2) as i:
                for u in range(2):
                    affine2(2 * i + (2 + u), u)

        @block.tensor
        def _(pe):
            def three(o, a, b, w, v, first, last):
                nc.tensor.matmul(o, a, w, start=first, stop=False)
                nc.tensor.matmul(o, a, v, start=False, stop=False)
                return nc.tensor.matmul(o, b, w, start=False, stop=last)

            def k_tile(x, par, kt):
                row = kt if kt < EK else 26 + kt - EK
                m = P if kt < EK + FT else SHARED if kt == EK + FT else WHOLE
                for h in range(2):
                    last = three(acc[par][:, h, :], x_hi[0:m, row, :], x_lo[0:m, row, :],
                                 w1_hi[0:m, kt, h * HALF:(h + 1) * HALF],
                                 w1_lo[0:m, kt, h * HALF:(h + 1) * HALF], kt == 0, kt == KT - 1)
                return last

            def transpose_group(x, g, first=False):
                a, b = GROUPS[g]
                n = 16 * 2 * (b - a)
                pe.wait_ge(gathered[g], n * x + n)
                if g > 0 or not first:
                    pe.wait_ge(ts_lo, NG * x + g)
                if g == 0 and not first:
                    pe.wait_ge(feat_done, x)
                    pe.wait_ge(f_lo, x)
                for kt in range(a, b):
                    o = (kt - a) * P
                    nc.tensor.transpose(tr[:, 0, o:o + P], xb[:, kt * P:(kt + 1) * P], ident[:, :])
                    last = nc.tensor.transpose(tr[0:DIM, 1, o:o + P], xb[:, kt * P + DIM:(kt + 1) * P], ident[:, :])
                last.then_inc(trans_ready, 1)

            def cont_cate(x):
                pe.wait_ge(ts_lo, NG * x + NG)
                for kt in range(EK):
                    n = 2 * CONT
                    last = three(tr[:, 0, kt * n:(kt + 1) * n], x_hi[:, kt, :], x_lo[:, kt, :],
                                 ebd_hi[:, :], ebd_lo[:, :], True, True)
                last.then_inc(c_ready, 1)

            x_dots = [t[0:DIM, 0:CATE, :].rearrange("p f (s j) -> p (f s) j", s=4) for t in (x_hi, x_lo)]

            def gram(x, q, first=False):
                if q >= 2 or not first:
                    pe.wait_ge((gram_act, gram_dve)[q % 2], 4 * x + q // 2)
                for c in range(4):
                    j = 4 * q + c
                    n = 4 * CATE
                    hi, lo = x_dots
                    last = three(gr[0:n, q % 2, c * n:(c + 1) * n], hi[:, :, j], lo[:, :, j],
                                 hi[:, :, j], lo[:, :, j], True, True)
                last.then_inc(gram_ready, 1)

            def transpose_features(x):
                pe.wait_ge(feat_done, x + 1)
                for s in range(FT):
                    nc.tensor.transpose(tr[:, 1, s * P:(s + 1) * P], feats[:, s * P:(s + 1) * P], ident[:, :])
                nc.tensor.transpose(tr[0:PART, 1, FT * P:(FT + 1) * P], feats[:, FT * P:PACKED],
                                    ident[:, :]).then_inc(f_trans, 1)

            pe.wait_ge(ident_ready, 2)
            pe.wait_ge(e13_in, 32)
            nc.tensor.transpose(tr[:, 0, 0:CONT], e13[:, :, :].rearrange("p a d -> p (a d)"),
                                ident[0:CONT, 0:CONT]).then_inc(eT_ready, 1)
            pe.wait_ge(vbd_ready, 1)
            nc.tensor.matmul(tr[:, 1, 0:NN], ones, ee, start=True, stop=True).then_inc(s_ready, 1)
            for n in range(V_TILES):
                m = min(P, CONT * DIM - n * P)
                pe.wait_ge(*staged(n))
                for h in range(2):
                    last = nc.tensor.matmul(acc[1][0:CONT, h, :], vbd[0:m, n, :],
                                            stage[0:m, n % STAGES, h * HALF:(h + 1) * HALF],
                                            start=n == 0, stop=n == V_TILES - 1)
                last.then_inc(v_free, 1)
            pe.wait_ge(setup_done, 1)
            for g in range(NG):
                transpose_group(0, g, first=True)
            cont_cate(0)
            for q in range(FILLS):
                gram(0, q, first=True)
            transpose_features(0)

            def iteration(x, par, first=False, last=False):
                if not isinstance(x, int) or x >= 2:
                    pe.wait_ge(norm_act, x - 1)
                    pe.wait_ge(norm_dve, x - 1)
                for kt in range(KT):
                    if first:
                        pe.wait_ge(stage_free, kt + 1)
                    if kt == EK:
                        pe.wait_ge(f_lo, x + 1)
                    if kt == EK + FT:
                        pe.wait_ge(late_done, x + 1)
                    done = k_tile(x, par, kt)
                    if kt == KT - 1:
                        done.then_inc(acc_ready, 1)
                    if last:
                        if kt == 2 * K2 - 1:
                            done.then_inc(w1_free, 1)
                        continue
                    for g, (a, b) in enumerate(GROUPS):
                        if kt == b - 1:
                            transpose_group(x + 1, g)
                    if kt == EK + 1:
                        cont_cate(x + 1)
                    if kt >= EK + 2:
                        for q in range(2):
                            gram(x + 1, 2 * (kt - EK - 2) + q)
                if not last:
                    transpose_features(x + 1)

            iteration(0, 0, first=True)
            iteration(1, 1)
            iteration(2, 0)
            with pe.Fori(0, (TILES - 4) // 2) as i:
                for u in range(2):
                    iteration(2 * i + (3 + u), 1 - u)
            iteration(TILES - 1, 1, last=True)

            def transpose2(x, par):
                t = tr if par == 0 else gr
                pe.wait_ge(h1_in[par], 8 * x + 16 - 8 * par)
                if not isinstance(x, int) or x >= 2:
                    pe.wait_ge(y_ready, K2 * (x - 1))
                for k in range(K2):
                    last = nc.tensor.transpose(t[:, k // 4, (k % 4) * P:(k % 4 + 1) * P],
                                               h1[:, par, k * P:(k + 1) * P], ident[:, :])
                last.then_inc(t2_ready, 1)

            def product2(x, par, first=False, last=False):
                if not isinstance(x, int) or x >= 2:
                    pe.wait_ge(h2_done, x - 1)
                pe.wait_ge(y_split, x + 1)
                for k in range(K2):
                    if first:
                        pe.wait_ge(w2_done, k + 1)
                    for h in range(2):
                        done = three(acc[par][:, h, :], y_hi[:, par, k, :], y_lo[:, par, k, :],
                                     w2_hi[:, k, h * HALF:(h + 1) * HALF],
                                     w2_lo[:, k, h * HALF:(h + 1) * HALF], k == 0, k == K2 - 1)
                    if k == 3 and not last:
                        transpose2(x + 1, 1 - par)
                done.then_inc(acc2_ready, 1)

            transpose2(0, 0)
            product2(0, 0, first=True)
            product2(1, 1)
            with pe.Fori(0, (TILES - 4) // 2) as i:
                for u in range(2):
                    product2(2 * i + (2 + u), u)
            product2(TILES - 2, 0)
            product2(TILES - 1, 1, last=True)

        @block.scalar
        def _(act):
            act.dma_start(rows_sb[:, :], rows.bitcast(U32)).then_inc(rows_in, 16)
            with nc.allow_non_contiguous_dma(reason="a parameter to each partition"):
                act.dma_start(g1_col[:, :], g1.rearrange("(n p) -> p n", p=P)).then_inc(g1_in, 16)
                act.dma_start(be1_col[:, :], be1.rearrange("(n p) -> p n", p=P)).then_inc(g1_in, 16)
            act.dma_start(bout_bc[:, :], bout.unsqueeze(0).to_broadcast([P, 1])).then_inc(g1_in, 16)

            def split_group(x, g):
                a, b = GROUPS[g]
                n = (b - a) * P
                act.wait_ge(trans_ready, NG * x + g + 1)
                nc.scalar.copy(x_hi[:, a:b, :].rearrange("p k b -> p (k b)"), tr[:, 0, 0:n]).then_inc(ts_hi, 1)
                nc.scalar.copy(x_hi[0:DIM, EK + a:EK + b, :].rearrange("p k b -> p (k b)"),
                               tr[0:DIM, 1, 0:n]).then_inc(ts_hi, 1)

            def take_dots(x, q, first=False):
                act.wait_ge(gram_ready, FILLS * x + q + 1)
                if q < 2 and not first:
                    act.wait_ge(dots_out, 64 * x)
                src = gr[0:4 * CATE, 0, 0:16 * CATE].rearrange("p (c g t) -> p t g c", c=4, g=CATE)
                nc.scalar.copy(dots[:, :, :, 4 * q:4 * q + 4], src).then_inc(gram_act, 1)

            def features(x, first=False):
                act.wait_ge(f_trans, x + 1)
                if not first:
                    act.wait_ge(late_done, x)
                nc.scalar.copy(x_hi[:, 26:26 + FT, :].rearrange("p k b -> p (k b)"), tr[:, 1, 0:FT * P])
                nc.scalar.copy(late[0:PART, 0, :], tr[0:PART, 1, FT * P:(FT + 1) * P]).then_inc(f_hi, 1)

            def norm1(x, par):
                act.wait_ge(ln, LN_STEPS * x + 3)
                nc.scalar.activation(st[:, 1:2], st[:, 0:1], ACT.Sqrt).then_inc(sqrt_done, 1)
                act.wait_ge(ln, LN_STEPS * x + 8)
                if not isinstance(x, int) or x >= 2:
                    act.wait_ge(h1_out[par], 8 * x - 8 * par)
                nc.scalar.activation(stage[:, par, 0:HALF], acc[par][:, 0, :], ACT.Identity,
                                     bias=st[:, 7:8], scale=st[:, 6:7]).then_inc(norm_act, 1)

            def w1_hi_part(k):
                n = V_TILES + k
                m = P if k < EK + FT else SHARED if k == EK + FT else WHOLE
                act.wait_ge(*staged(n))
                if k == EK + FT:
                    act.wait_ge(b1_in, 16)
                    act.wait_ge(v_free, V_TILES)
                    nc.scalar.copy(stage[V_AT:V_AT + CONT, n % STAGES, :],
                                   acc[1][0:CONT, :, :].rearrange("p h n -> p (h n)")).then_inc(v_in, 1)
                    act.wait_ge(v_in, 1)
                nc.scalar.copy(w1_hi[0:m, k, :], stage[0:m, n % STAGES, :]).then_inc(stage_hi, 1)

            split_group(0, 0)
            split_group(0, 1)
            for k in range(0, 3):
                w1_hi_part(k)
            split_group(0, 2)
            for k in range(3, 6):
                w1_hi_part(k)
            split_group(0, 3)
            for q in range(0, FILLS, 2):
                w1_hi_part(6 + q // 2)
                take_dots(0, q, first=True)
            features(0, first=True)
            for k in range(10, EK):
                w1_hi_part(k)

            def iteration(x, par, first=False):
                if not first:
                    norm1(x - 1, 1 - par)
                for g in range(NG):
                    split_group(x + 1, g)
                if first:
                    for k in range(EK, KT):
                        w1_hi_part(k)
                for q in range(0, FILLS, 2):
                    take_dots(x + 1, q)
                features(x + 1)

            iteration(0, 0, first=True)
            iteration(1, 1)
            iteration(2, 0)
            with act.Fori(0, (TILES - 4) // 2) as i:
                for u in range(2):
                    iteration(2 * i + (3 + u), 1 - u)
            norm1(TILES - 2, 0)

            def relu1(x, par):
                t = tr if par == 0 else gr
                act.wait_ge(t2_ready, x + 1)
                if not isinstance(x, int) or x >= 1:
                    act.wait_ge(y_split, x)
                for k in range(K2):
                    nc.scalar.activation(y[:, k, :], t[:, k // 4, (k % 4) * P:(k % 4 + 1) * P], ACT.Relu,
                                         bias=be1_col[:, k:k + 1], scale=g1_col[:, k:k + 1]).then_inc(y_ready, 1)

            def norm2(x, par):
                act.wait_ge(ln, LN_STEPS * x + (LN_STEPS * TILES + 3))
                nc.scalar.activation(st[:, 1:2], st[:, 0:1], ACT.Sqrt).then_inc(sqrt_done, 1)
                act.wait_ge(ln, LN_STEPS * x + (LN_STEPS * TILES + 8))
                if not isinstance(x, int) or x >= 2:
                    act.wait_ge(a2_mul, x - 1)
                nc.scalar.activation(n2[:, par, :], h2[:, :], ACT.Identity,
                                     bias=st[:, 7:8], scale=st[:, 6:7]).then_inc(n2_ready, 1)

            def w2_hi_part(k):
                b = (k + 2) % STAGES
                act.wait_ge(w2_in[b], 16 * (k // STAGES + 1))
                nc.scalar.copy(w2_hi[:, k, :], stage[:, b, :]).then_inc(w2_hi_done, 1)

            act.wait_ge(w1_free, 1)
            for k in range(2):
                w2_hi_part(k)
            norm1(TILES - 1, 1)
            act.wait_ge(acc_ready, TILES)
            act.wait_ge(g1_in, 48)
            relu1(0, 0)
            for k in range(2, K2):
                w2_hi_part(k)
            relu1(1, 1)
            norm2(0, 0)
            relu1(2, 0)
            with act.Fori(0, (TILES - 4) // 2) as i:
                for u in range(2):
                    norm2(2 * i + (1 + u), 1 - u)
                    relu1(2 * i + (3 + u), 1 - u)
            norm2(TILES - 3, 1)
            relu1(TILES - 1, 1)
            norm2(TILES - 2, 0)
            norm2(TILES - 1, 1)
            act.wait_ge(logit_done, TILES)
            nc.scalar.activation(prob[:, :], logit[:, :], ACT.Sigmoid, bias=bout_bc[:, 0:1]).then_inc(prob_done, 1)

        @block.vector
        def _(dve):
            TT = nc.vector.tensor_tensor
            TS = nc.vector.tensor_scalar
            STT = nc.vector.scalar_tensor_tensor
            done = [0]

            def step(ins):
                done[0] += 1
                ins.then_inc(setup, 1)

            step(nc.vector.memset(ebd[:, :], 0.0))
            step(nc.vector.memset(vbd[:, :, :], 0.0))
            step(nc.vector.memset(ones, 1.0))
            dve.wait_ge(eT_ready, 1)
            step(nc.vector.tensor_copy(eT[:, :], tr[:, 0, 0:CONT]))
            dve.wait_ge(setup, done[0])
            vflat = vbd[:, :, :].rearrange("p n i -> p (n i)")
            hop = CONT + 2
            nc.vector.tensor_copy(vflat[0:DIM, 0::hop], eT[0:DIM, 0::2])
            nc.vector.tensor_copy(vflat[DIM:P, 1::hop], eT[DIM:P, 1::2])
            for k in range(1, CONT // 2 + 1):
                o = (k - 1) * CONT
                TT(ee[:, o:o + CONT - k], eT[0:DIM, 0:CONT - k], eT[0:DIM, k:CONT], ALU.mult)
                last = TT(ee[:, o + CONT - k:o + CONT], eT[0:DIM, CONT - k:CONT], eT[0:DIM, 0:k], ALU.mult)
            last.then_inc(vbd_ready, 1)
            nc.vector.tensor_copy(ebd[0:DIM, 0:CONT], eT[0:DIM, :])
            step(nc.vector.tensor_copy(ebd[DIM:P, CONT:2 * CONT], eT[DIM:P, :]))
            dve.wait_ge(setup, done[0])
            step(nc.vector.tensor_copy(ebd_hi[:, :], ebd[:, :]))
            dve.wait_ge(setup, done[0])
            TT(ebd_lo[:, :], ebd[:, :], ebd_hi[:, :].bitcast(F32), ALU.subtract)

            nc.vector.memset(feats[:, PACKED - 1:PACKED], 1.0)
            dve.wait_ge(s_ready, 1)
            nc.vector.tensor_copy(cc_dots[:, :], tr[:, 1, 0:NN]).then_inc(setup_done, 1)

            def split_group(x, g):
                a, b = GROUPS[g]
                n = (b - a) * P
                dve.wait_ge(ts_hi, 2 * NG * x + 2 * g + 1)
                TT(x_lo[:, a:b, :].rearrange("p k b -> p (k b)"), tr[:, 0, 0:n],
                   x_hi[:, a:b, :].rearrange("p k b -> p (k b)").bitcast(F32), ALU.subtract)
                dve.wait_ge(ts_hi, 2 * NG * x + 2 * g + 2)
                TT(x_lo[0:DIM, EK + a:EK + b, :].rearrange("p k b -> p (k b)"), tr[0:DIM, 1, 0:n],
                   x_hi[0:DIM, EK + a:EK + b, :].rearrange("p k b -> p (k b)").bitcast(F32),
                   ALU.subtract).then_inc(ts_lo, 1)

            def w1_lo_part(k):
                n = V_TILES + k
                m = P if k < EK + FT else SHARED if k == EK + FT else WHOLE
                dve.wait_ge(stage_hi, k + 1)
                TT(w1_lo[0:m, k, :], stage[0:m, n % STAGES, :], w1_hi[0:m, k, :].bitcast(F32),
                   ALU.subtract).then_inc(stage_free, 1)

            def packed_features(x, par):
                dve.wait_ge(conts_in[par], 16 * x + 32 - 16 * par)
                if not isinstance(x, int) or x >= 1:
                    dve.wait_ge(f_trans, x)
                nc.vector.tensor_copy(feats[:, CC + NN:PACKED - 1], c2[:, par, 0:CONT])
                for k in range(1, CONT // 2 + 1):
                    last = TT(feats[:, CC + (k - 1) * CONT:CC + k * CONT], c2[:, par, 0:CONT],
                              c2[:, par, k:k + CONT], ALU.mult)
                last.then_inc(cc_done, 1)
                dve.wait_ge(cc_done, x + 1)
                TT(feats[:, CC:CC + NN], feats[:, CC:CC + NN], cc_dots[:, :], ALU.mult)
                dve.wait_ge(c_ready, x + 1)
                TT(feats[:, 0:CC].rearrange("p (i g) -> p i g", i=CONT),
                   tr[:, 0, 0:CC].rearrange("p (g i) -> p i g", i=CONT),
                   c2[:, par, 0:CONT].unsqueeze(2).to_broadcast([P, CONT, CATE]), ALU.mult).then_inc(feat_done, 1)

            def take_dots(x, q, first=False):
                dve.wait_ge(gram_ready, FILLS * x + q + 1)
                if q < 2 and not first:
                    dve.wait_ge(dots_out, 64 * x)
                src = gr[0:4 * CATE, 1, 0:16 * CATE].rearrange("p (c g t) -> p t g c", c=4, g=CATE)
                nc.vector.tensor_copy(dots[:, :, :, 4 * q:4 * q + 4], src).then_inc(gram_dve, 1)

            def features_lo(x):
                dve.wait_ge(f_hi, x + 1)
                TT(x_lo[:, 26:26 + FT, :].rearrange("p k b -> p (k b)"), tr[:, 1, 0:FT * P],
                   x_hi[:, 26:26 + FT, :].rearrange("p k b -> p (k b)").bitcast(F32),
                   ALU.subtract).then_inc(f_lo, 1)

            def late_features(x):
                dve.wait_ge(late_in, 16 * DIAGS * x + 16 * DIAGS)
                dve.wait_ge(f_hi, x + 1)
                r = 26 + FT
                nc.vector.tensor_copy(x_hi[0:SHARED, r, :], late[0:SHARED, 0, :])
                nc.vector.tensor_copy(x_hi[0:WHOLE, r + 1:r + 3, :], late[0:WHOLE, 1:3, :]).then_inc(late_hi, 1)
                dve.wait_ge(late_hi, x + 1)
                TT(x_lo[0:SHARED, r, :], late[0:SHARED, 0, :], x_hi[0:SHARED, r, :].bitcast(F32), ALU.subtract)
                TT(x_lo[0:WHOLE, r + 1:r + 3, :], late[0:WHOLE, 1:3, :],
                   x_hi[0:WHOLE, r + 1:r + 3, :].bitcast(F32), ALU.subtract).then_inc(late_done, 1)

            def layer_norm(x, rows, used):
                b = LN_STEPS * x
                for h in range(2):
                    last = nc.vector.bn_stats(bn[:, h, :], rows[:, h, :])
                last.then_inc(ln, 1)
                dve.wait_ge(ln, b + 1)
                stands_alone(dve)
                nc.vector.bn_aggr(mv[:, :], bn[:, :, :].rearrange("p h s -> p (h s)")).then_inc(ln, 1)
                dve.wait_ge(ln, b + 2)
                TS(st[:, 0:1], mv[:, 1:2], EPS, None, ALU.add).then_inc(ln, 1)
                dve.wait_ge(sqrt_done, x + 1)
                nc.vector.reciprocal(st[:, 2:3], st[:, 1:2]).then_inc(ln, 1)
                dve.wait_ge(ln, b + 4)
                STT(st[:, 3:4], st[:, 2:3], st[:, 2:3], st[:, 0:1], ALU.mult, ALU.mult).then_inc(ln, 1)
                dve.wait_ge(ln, b + 5)
                TS(st[:, 4:5], st[:, 3:4], -0.5, 1.5, ALU.mult, ALU.add).then_inc(ln, 1)
                dve.wait_ge(ln, b + 6)
                if used is not None:
                    dve.wait_ge(*used)
                TT(st[:, 6:7], st[:, 2:3], st[:, 4:5], ALU.mult).then_inc(ln, 1)
                dve.wait_ge(ln, b + 7)
                STT(st[:, 7:8], mv[:, 0:1], -1.0, st[:, 6:7], ALU.mult, ALU.mult).then_inc(ln, 1)

            def norm1(x, par):
                dve.wait_ge(acc_ready, x + 1)
                first = isinstance(x, int) and x == 0
                layer_norm(x, acc[par], None if first else (norm_act, x))
                if not isinstance(x, int) or x >= 2:
                    dve.wait_ge(h1_out[par], 8 * x - 8 * par)
                TS(stage[:, par, HALF:HID], acc[par][:, 1, :], mv[:, 0:1], st[:, 6:7],
                   ALU.subtract, ALU.mult).then_inc(norm_dve, 1)

            split_group(0, 0)
            split_group(0, 1)
            for k in range(0, 3):
                w1_lo_part(k)
            split_group(0, 2)
            for k in range(3, 6):
                w1_lo_part(k)
            split_group(0, 3)
            packed_features(0, 0)
            for q in range(1, FILLS, 2):
                w1_lo_part(6 + q // 2)
                take_dots(0, q, first=True)
            features_lo(0)
            for k in range(10, EK):
                w1_lo_part(k)

            def iteration(x, par, first=False):
                if not first:
                    norm1(x - 1, 1 - par)
                split_group(x + 1, 0)
                split_group(x + 1, 1)
                late_features(x)
                split_group(x + 1, 2)
                split_group(x + 1, 3)
                if first:
                    for k in range(EK, KT):
                        w1_lo_part(k)
                packed_features(x + 1, 1 - par)
                for q in range(1, FILLS, 2):
                    take_dots(x + 1, q)
                features_lo(x + 1)

            iteration(0, 0, first=True)
            iteration(1, 1)
            iteration(2, 0)
            with dve.Fori(0, (TILES - 4) // 2) as i:
                for u in range(2):
                    iteration(2 * i + (3 + u), 1 - u)
            norm1(TILES - 2, 0)
            late_features(TILES - 1)

            def w2_lo_part(k):
                b = (k + 2) % STAGES
                dve.wait_ge(w2_hi_done, k + 1)
                TT(w2_lo[:, k, :], stage[:, b, :], w2_hi[:, k, :].bitcast(F32), ALU.subtract).then_inc(w2_done, 1)

            def split_y(x, par):
                dve.wait_ge(y_ready, K2 * x + K2)
                if not isinstance(x, int) or x >= 2:
                    dve.wait_ge(acc2_ready, x - 1)
                nc.vector.tensor_copy(y_hi[:, par, :, :], y[:, :, :]).then_inc(y_hi_done, 1)
                dve.wait_ge(y_hi_done, x + 1)
                TT(y_lo[:, par, :, :], y[:, :, :], y_hi[:, par, :, :].bitcast(F32), ALU.subtract).then_inc(y_split, 1)

            def norm2(x, par):
                dve.wait_ge(acc2_ready, x + 1)
                if not isinstance(x, int) or x >= 1:
                    dve.wait_ge(n2_ready, x)
                TT(h2[:, :].rearrange("p (h n) -> p h n", h=2), acc[par][:, :, :],
                   b2_bc[:, :].rearrange("p (h n) -> p h n", h=2), ALU.add).then_inc(h2_done, 1)
                dve.wait_ge(h2_done, x + 1)
                layer_norm(x + TILES, h2[:, :].rearrange("p (h n) -> p h n", h=2), None)

            def product_out(x, par):
                dve.wait_ge(a2_ready, x + 1)
                if not isinstance(x, int) or x >= 1:
                    dve.wait_ge(logit_done, x)
                STT(r2[:, :], a2[:, par, :], 0.0, wout_bc[:, :], ALU.max, ALU.mult,
                    accum_out=logit[:, at(x)]).then_inc(logit_done, 1)

            for k in range(2):
                w2_lo_part(k)
            norm1(TILES - 1, 1)
            dve.wait_ge(acc_ready, TILES)
            split_y(0, 0)
            for k in range(2, K2):
                w2_lo_part(k)
            split_y(1, 1)
            dve.wait_ge(par_in, 16 * 4)
            norm2(0, 0)
            split_y(2, 0)
            with dve.Fori(0, (TILES - 4) // 2) as i:
                for u in range(2):
                    norm2(2 * i + (1 + u), 1 - u)
                    split_y(2 * i + (3 + u), 1 - u)
                    product_out(2 * i + u, u)
            norm2(TILES - 3, 1)
            split_y(TILES - 1, 1)
            product_out(TILES - 4, 0)
            norm2(TILES - 2, 0)
            product_out(TILES - 3, 1)
            norm2(TILES - 1, 1)
            product_out(TILES - 2, 0)
            product_out(TILES - 1, 1)


_INS = ["r_conts", "r_cates", "L0_rec_emb_table", "L0_rec_W1", "L0_rec_b1", "L0_rec_ln1_g", "L0_rec_ln1_b",
        "L0_rec_W2", "L0_rec_b2", "L0_rec_ln2_g", "L0_rec_ln2_b", "L0_rec_Wout", "L0_rec_bout"]


def kernel(**inputs):
    import concourse.bacc as bacc
    from concourse.bass_utils import run_bass_kernel_spmd

    nc = bacc.Bacc("TRN2", target_bir_lowering=False, num_devices=1, dynamic_dma_scratch_size=2048)
    arrays, args = {}, []
    for name in _INS:
        a = np.ascontiguousarray(inputs[name])
        arrays[f"in_{name}"] = a
        args.append(nc.dram_tensor(f"in_{name}", a.shape, mybir.dt.from_np(a.dtype), kind="ExternalInput").ap())
    arrays["feature_rows"] = feature_rows()
    args.append(nc.dram_tensor("feature_rows", (P, FK), I32, kind="ExternalInput").ap())
    args.append(nc.dram_tensor("out", (BATCH, 1), F32, kind="ExternalOutput").ap())
    build(nc, *args)
    r = run_bass_kernel_spmd(nc, [arrays], core_ids=[0])
    return r.results[0]["out"]
```

```python
from contextlib import ExitStack

import numpy as np
import concourse.bass as bass
from concourse import mybir

F32 = mybir.dt.float32
F32R = mybir.dt.float32r
I32 = mybir.dt.int32
U32 = mybir.dt.uint32
ALU = mybir.AluOpType
ACT = mybir.ActivationFunctionType

P = 128
BATCH = 2048
TILES = BATCH // P
CONT = 13
CATE = 26
FIELDS = CONT + CATE
DIM = 64
VOCAB = 12500
HID = 1024
HALF = HID // 2
EPS = 1e-5
PAIR_ROW0 = FIELDS * DIM
EK = CATE * DIM // P
CC = CONT * CATE
NN = CONT * (CONT - 1) // 2
PACKED = CC + NN + CONT + 1
FT = 3
PART = PACKED - FT * P
V_AT = PART - 1 - CONT
DIAG = 25
DIAGS = 13
SHARED = PART + 3 * DIAG
WHOLE = 5 * DIAG
WIN = P + 2 * CONT + P - 2
FAC_AT = CC % P
FAC = FAC_AT + NN + CONT + 1
FK = 6
KT = EK + FK
F_ROW = CATE
K2 = HID // P
W2_AT = 4
GROUPS = ((0, 4), (4, 7), (7, 10), (10, 13))
NG = len(GROUPS)
QUAD = 32
FILLS = 16
PER_FILL = 2
G_ROW = CATE * QUAD
G_WRAP = (CATE * CATE - 1) * QUAD
G_AGAIN = DIAGS - 1
G_PITCH = (CATE + DIAGS) * G_ROW
LATE_IN = (32 * 3, 32 * 10)
V_TILES = (CONT + 1) // 2
IN_FLIGHT = 4
SPLIT_K = (((), (0, 1, 2, 3), (4, 5, 6), (7, 8, 9)), ((10,), (11, 12), (13, 14, 15), (16, 17, 18)))
USE_K = (((), (0, 1, 2, 3), (4, 5, 6), (7,)), ((10,), (11,), (12, 13), (14,)))


def field_of(f):
    return 2 * f if f < EK else 2 * (f - EK) + 1


def pair_row(i, j):
    i, j = min(i, j), max(i, j)
    return PAIR_ROW0 + i * FIELDS - i * (i + 1) // 2 + (j - i - 1)


def feature_rows():
    rows = np.zeros((P, FK), np.int32)
    packed = [pair_row(i, CONT + g) for g in range(CATE) for i in range(CONT)]
    packed += [pair_row(i, (i + k) % CONT) for k in range(1, CONT // 2 + 1) for i in range(CONT)]
    packed += [0] * (CONT + 1)
    for c, r in enumerate(packed):
        rows[c % P, c // P] = r
    for k in range(1, DIAGS + 1):
        for f in range(DIAG):
            a, b = (f, f + k) if f + k < CATE else (f + 1, f + k - CATE)
            slot, at = diag_place(k)
            rows[at + f, slot] = pair_row(CONT + field_of(a), CONT + field_of(b))
    return rows


def diag_place(k):
    if k <= 5:
        return 4, DIAG * (k - 1)
    if k <= 10:
        return 5, DIAG * (k - 6)
    return 3, PART + DIAG * (k - 11)


def build(nc, conts, cates, emb, W1, b1, g1, be1, W2, b2, g2, be2, Wout, bout, rows, out):
    h1_dram = nc.dram_tensor("h1_scratch", (P, TILES, HID), F32, kind="Internal").ap()
    dots_dram = nc.dram_tensor("dots_scratch", (4, G_PITCH), F32, kind="Internal").ap()

    with ExitStack() as memory:
        def sb(name, shape, dt=F32, ctx=memory):
            return ctx.enter_context(nc.sbuf_tensor(name, shape, dt))

        def sem(name):
            return memory.enter_context(nc.semaphore(name))

        raw = ExitStack()
        raw_hi = [sb(f"raw_hi{k}", [P, HID], F32, raw) for k in range(KT)]
        raw_lo = [sb(f"raw_lo{k}", [P, HID], F32, raw) for k in range(KT)]
        raw.close()
        w1_hi = sb("w1_hi", [P, KT, HID], F32R)
        w1_lo = sb("w1_lo", [P, KT, HID], F32R)
        x_both = sb("x_both", [P, 2, 32, P], F32R)
        x_hi, x_lo = x_both[:, 0, :, :], x_both[:, 1, :, :]
        xb = sb("xb", [P, CATE * DIM])
        dots = sb("dots", [4 * CATE, 4, CATE, QUAD])
        feats = sb("feats", [P, PACKED])
        late = sb("late", [P, 3, P])
        late_t = sb("late_t", [P, 3, P])
        h1_row = sb("h1_row", [P, HID])
        c2 = sb("c2", [P, 2, 2 * CONT])
        cates_sb = sb("cates_sb", [P, 2, CATE], I32)
        shift = sb("shift", [P, CATE])
        cates_f = sb("cates_f", [P, CATE])
        idx = sb("idx", [P, 2, CATE], U32)
        rows_sb = sb("rows_sb", [P, FK], U32)
        eT = sb("eT", [P, CONT])
        vbd = sb("vbd", [P, V_TILES, CONT])
        win_hi = sb("win_hi", [P, WIN], F32R)
        win_lo = sb("win_lo", [P, WIN], F32R)
        fac = sb("fac", [P, 2])
        cc_dots = sb("cc_dots", [P, FT * P])
        ident = sb("ident", [P, P])
        bn = sb("bn", [P, 2, 6])
        mv = sb("mv", [P, 2])
        st = sb("st", [P, 8])
        logit = sb("logit", [P, TILES])
        prob = sb("prob", [P, TILES])
        bout_bc = sb("bout_bc", [P, 1])
        g1_col = sb("g1_col", [P, K2])
        be1_col = sb("be1_col", [P, K2])
        ee = late[0:DIM, 0:2, :].rearrange("p k b -> p (k b)")[:, 0:FAC]
        ones = feats[0:DIM, PACKED - 1:PACKED]
        e13 = late[0:CONT, 2, :].rearrange("p (a d) -> p a d", a=2)

        y_hi = w1_hi[:, 0:2, :].rearrange("p a (k b) -> p a k b", k=K2)
        y_lo = w1_lo[:, 0:2, :].rearrange("p a (k b) -> p a k b", k=K2)
        h1 = raw_hi[2:4]
        y = raw_lo[2][:, :].rearrange("p (k b) -> p k b", k=K2)
        h2 = raw_lo[3][:, :]
        w2_hi, w2_lo = w1_hi[:, W2_AT:W2_AT + K2, :], w1_lo[:, W2_AT:W2_AT + K2, :]
        n2 = raw_lo[12:14]
        a2 = raw_lo[14:16]
        r2 = raw_lo[16][:, :]
        b2_bc, g2_bc, be2_bc, wout_bc = [raw_hi[k][:, :] for k in range(12, 16)]

        def pb(name):
            return memory.enter_context(nc.psum_tensor(name, [P, 2, HALF], F32))

        acc = [pb("acc0"), pb("acc1")]
        tr = pb("tr")
        gr = pb("gr")

        cates_in = [sem("cates_in0"), sem("cates_in1")]
        conts_in = [sem("conts_in0"), sem("conts_in1")]
        e13_in = sem("e13_in")
        rows_in = sem("rows_in")
        idx_step = sem("idx_step")
        ident_ready = sem("ident_ready")
        w1_in = [sem(f"w1_in{k}") for k in range(KT)]
        v_rows_in = [sem(f"v_rows_in{n}") for n in range(V_TILES)]
        b1_in = sem("b1_in")
        v_in = sem("v_in")
        w1_rounded = sem("w1_rounded")
        w1_split = sem("w1_split")
        v_done = sem("v_done")
        eT_ready = sem("eT_ready")
        setup = sem("setup")
        vbd_ready = sem("vbd_ready")
        s_ready = sem("s_ready")
        setup_done = sem("setup_done")
        gathered = [sem(f"gathered{g}") for g in range(NG)]
        trans_ready = sem("trans_ready")
        ts_hi = sem("ts_hi")
        ts_lo = sem("ts_lo")
        factors = sem("factors")
        f_trans = sem("f_trans")
        cc_sum = sem("cc_sum")
        factors_t = sem("factors_t")
        feat_done = sem("feat_done")
        f_used = sem("f_used")
        f_hi = sem("f_hi")
        f_lo = sem("f_lo")
        gram_ready = sem("gram_ready")
        gram_half = sem("gram_half")
        gram_taken = sem("gram_taken")
        dots_out = sem("dots_out")
        late_in = [sem("late_in0"), sem("late_in1")]
        late_sum = [sem("late_sum0"), sem("late_sum1")]
        late_hi = [sem("late_hi0"), sem("late_hi1")]
        late_done = [sem("late_done0"), sem("late_done1")]
        acc_ready = sem("acc_ready")
        w1_free = sem("w1_free")
        ln = sem("ln")
        sqrt_done = sem("sqrt_done")
        norm_act = sem("norm_act")
        norm_dve = sem("norm_dve")
        h1_out = sem("h1_out")
        w2_in = [sem(f"w2_in{k}") for k in range(K2)]
        w2_hi_done = sem("w2_hi_done")
        w2_done = sem("w2_done")
        g1_in = sem("g1_in")
        par_in = sem("par_in")
        h1_in = [sem("h1_in0"), sem("h1_in1")]
        t2_ready = sem("t2_ready")
        y_ready = sem("y_ready")
        y_hi_done = sem("y_hi_done")
        y_split = sem("y_split")
        acc2_ready = sem("acc2_ready")
        h2_done = sem("h2_done")
        n2_ready = sem("n2_ready")
        a2_mul = sem("a2_mul")
        a2_ready = sem("a2_ready")
        logit_done = sem("logit_done")
        prob_done = sem("prob_done")
        out_done = sem("out_done")
        passed = sem("passed")

        LN_STEPS = 8

        def at(x):
            return slice(x, x + 1) if isinstance(x, int) else bass.ds(x, 1)

        block = memory.enter_context(nc.Block())

        def stands_alone(eng):
            eng.sem_inc(passed, 1)

        def rows_of(k):
            return P if k < EK + FT else SHARED if k == EK + FT else WHOLE

        def cc_bank(t):
            return tr[:, 1, 2 * P * t:2 * P * (t + 1)] if t < 2 else gr[:, 1, 0:2 * P]

        def gram_part(q, part):
            bank = (gr, tr)[q // 2 % 2][0:4 * CATE, q % 2, 0:PER_FILL * 8 * CATE]
            return bank.rearrange("p (c h g t) -> p h t g c", c=PER_FILL, h=2, g=CATE)[:, part]

        def sums2(x, par):
            return acc[0] if isinstance(x, int) and x == 0 else acc[1 - par]

        def load_h1(eng, x, par):
            if not isinstance(x, int) or x >= 2:
                eng.wait_ge(t2_ready, x - 1)
                stands_alone(eng)
            eng.dma_start(h1[par][:, :], h1_dram[:, at(x), :].rearrange("p o n -> p (o n)")).then_inc(h1_in[par], 16)

        def v_rows(n):
            m = min(P, CONT * DIM - n * P)
            return raw_hi[EK + n][0:m, :] if n < FK else h1_row[0:m, :]

        @block.sync
        def _(sp):
            sp.dma_start(e13[:, 0, :], emb[0:CONT, :]).then_inc(e13_in, 16)
            sp.dma_start(e13[:, 1, :], emb[0:CONT, :]).then_inc(e13_in, 16)
            loads = [(v_rows(n), n * P, v_rows_in[n]) for n in range(V_TILES)]
            loads += [(raw_lo[k][:, :], CONT * DIM + k * P, w1_in[k]) for k in range(EK)]
            for n, (to, row, landed) in enumerate(loads):
                if n >= IN_FLIGHT:
                    sp.wait_ge(loads[n - IN_FLIGHT][2], 16)
                sp.dma_start(to, W1[row:row + to.shape[0], :]).then_inc(landed, 16)

            def dots_round_trip(x):
                sp.wait_ge(gram_taken, FILLS * x + FILLS)
                stands_alone(sp)
                for n in range(2):
                    sp.wait_ge(late_in[n], LATE_IN[n] * x)
                    stands_alone(sp)
                for s in range(4):
                    src = dots[s::4, s, :, :]
                    sp.dma_start(dots_dram[s, 0:CATE * G_ROW].rearrange("(f n) -> f n", n=G_ROW),
                                 src.rearrange("p g j -> p (g j)")).then_inc(dots_out, 16)
                    again = dots_dram[s, G_WRAP:G_WRAP + G_AGAIN * G_ROW].rearrange("(f n) -> f n", n=G_ROW)
                    sp.dma_start(again[:, QUAD:], src[0:G_AGAIN, 1:, :].rearrange("p g j -> p (g j)")
                                 ).then_inc(dots_out, 16)
                sp.wait_ge(dots_out, 128 * x + 128)
                for n in range(2):
                    sp.wait_ge(late_done[n], x)
                    stands_alone(sp)
                step = G_ROW + QUAD
                for k in (11, 12, 13, *range(1, 11)):
                    slot, row = diag_place(k)
                    for buf, base in ((late, k * QUAD), (late_t, k * G_ROW)):
                        src = dots_dram[:, base:base + DIAG * step]
                        src = src.rearrange("s (f n) -> f s n", n=step)[:, :, 0:QUAD]
                        dst = buf[row:row + DIAG, slot - FT, :].rearrange("p (s j) -> p s j", s=4)
                        sp.dma_start(dst, src).then_inc(late_in[k <= 10], 16)

            sp.wait_ge(w1_in[EK + FT], 16)
            sp.dma_start(raw_lo[EK + FT][PART - 1:PART, :], b1.unsqueeze(0)).then_inc(b1_in, 16)
            for x in range(4):
                dots_round_trip(x)
            with sp.Fori(0, (TILES - 4) // 2) as i:
                for u in range(2):
                    dots_round_trip(2 * i + (4 + u))

            sp.wait_ge(w1_free, 16)
            sp.dma_start(b2_bc, b2.unsqueeze(0).to_broadcast([P, HID])).then_inc(par_in, 16)
            sp.dma_start(g2_bc, g2.unsqueeze(0).to_broadcast([P, HID])).then_inc(par_in, 16)
            sp.dma_start(be2_bc, be2.unsqueeze(0).to_broadcast([P, HID])).then_inc(par_in, 16)
            sp.dma_start(wout_bc, Wout.rearrange("n o -> o n").to_broadcast([P, HID])).then_inc(par_in, 16)
            sp.wait_ge(h1_out, 16 * (TILES - 1))
            with sp.Fori(0, (TILES - 4) // 2) as i:
                for u in range(2):
                    load_h1(sp, 2 * i + (2 + u), u)
            load_h1(sp, TILES - 2, 0)
            sp.wait_ge(h1_out, 16 * TILES)
            load_h1(sp, TILES - 1, 1)
            sp.wait_ge(prob_done, 1)
            sp.dma_start(out.rearrange("(p x) o -> p (x o)", x=TILES), prob[:, :]).then_inc(out_done, 16)
            sp.wait_ge(out_done, 16)

        @block.gpsimd
        def _(pool):
            nc.gpsimd.memset(ident[:, :], 0.0).then_inc(ident_ready, 1)
            pool.wait_ge(ident_ready, 1)
            nc.gpsimd.affine_select(out=ident[:, :], in_=ident[:, :], compare_op=ALU.not_equal, fill=1.0,
                                    base=0, pattern=[[-1, P]], channel_multiplier=1).then_inc(ident_ready, 1)

            def gather(x, par, first=False):
                pool.wait_ge(idx_step, 4 * x + 4)
                stands_alone(pool)
                for g, (a, b) in enumerate(GROUPS):
                    if not first:
                        pool.wait_ge(trans_ready, NG * (x - 1) + g + 1)
                        stands_alone(pool)
                    for f in range(2 * a, 2 * b):
                        nc.gpsimd.indirect_dma_start(
                            out=xb[:, f * DIM:(f + 1) * DIM], out_offset=None, in_=emb,
                            in_offset=bass.IndirectOffsetOnAxis(ap=idx[:, par, f:f + 1], axis=0),
                        ).then_inc(gathered[g], 16)

            gather(0, 0, first=True)
            pool.wait_ge(rows_in, 16)
            for s in range(FK):
                m = rows_of(EK + s)
                nc.gpsimd.indirect_dma_start(
                    out=raw_lo[EK + s][0:m, :], out_offset=None, in_=W1,
                    in_offset=bass.IndirectOffsetOnAxis(ap=rows_sb[0:m, s:s + 1], axis=0),
                ).then_inc(w1_in[EK + s], 16)
            gather(1, 1)
            with pool.Fori(0, (TILES - 2) // 2) as i:
                for u in range(2):
                    gather(2 * i + (2 + u), u)

            def affine2(x, par):
                pool.wait_ge(n2_ready, x + 1)
                if not isinstance(x, int) or x >= 2:
                    pool.wait_ge(logit_done, x - 1)
                nc.gpsimd.tensor_tensor(a2[par][:, :], n2[par][:, :], g2_bc, ALU.mult).then_inc(a2_mul, 1)
                pool.wait_ge(a2_mul, x + 1)
                nc.gpsimd.tensor_tensor(a2[par][:, :], a2[par][:, :], be2_bc, ALU.add).then_inc(a2_ready, 1)

            pool.wait_ge(par_in, 16 * 4)
            for x in range(2):
                affine2(x, x)
            with pool.Fori(0, (TILES - 4) // 2) as i:
                for u in range(2):
                    affine2(2 * i + (2 + u), u)
            affine2(TILES - 2, 0)

        @block.tensor
        def _(pe):
            def three(o, a, b, w, v, first, last):
                nc.tensor.matmul(o, a, w, start=first, stop=False)
                nc.tensor.matmul(o, a, v, start=False, stop=False)
                return nc.tensor.matmul(o, b, w, start=False, stop=last)

            def half_k_tile(par, kt, h):
                row = kt if kt < EK else F_ROW + kt - EK
                m = rows_of(kt)
                return three(acc[par][:, h, :], x_hi[0:m, row, :], x_lo[0:m, row, :],
                             w1_hi[0:m, kt, h * HALF:(h + 1) * HALF],
                             w1_lo[0:m, kt, h * HALF:(h + 1) * HALF], kt == 0, kt == KT - 1)

            def transpose_group(x, g, first=False):
                a, b = GROUPS[g]
                n = 16 * 2 * (b - a)
                pe.wait_ge(gathered[g], n * x + n)
                if g > 0:
                    pe.wait_ge(ts_lo, NG * x + g)
                elif not first:
                    pe.wait_ge(gram_taken, FILLS * x)
                for kt in range(a, b):
                    last = nc.tensor.transpose(tr[:, 0, (kt - a) * P:(kt - a + 1) * P],
                                               xb[:, kt * P:(kt + 1) * P], ident[:, :])
                last.then_inc(trans_ready, 1)

            def cont_cate(x, g):
                pe.wait_ge(ts_lo, NG * x + g + 1)
                for kt in range(*GROUPS[g]):
                    row = 2 * CONT * kt
                    for t in range(row // P, (row + 2 * CONT - 1) // P + 1):
                        o = P - (row - t * P)
                        starts = row <= t * P
                        ends = t == FT - 1 and kt == EK - 1 or row + 2 * CONT >= (t + 1) * P
                        out_t = cc_bank(t)
                        parts = [(out_t, win_hi, x_both[:, :, kt, :]), (out_t[:, 0:P], win_lo, x_hi[:, kt, :])]
                        if ends:
                            parts.reverse()
                        for n, (to, win, moving) in enumerate(parts):
                            nc.tensor.matmul(to, win[:, o:o + P], moving, start=starts and n == 0,
                                             stop=ends and n == 1)

            def factor(x):
                pe.wait_ge(factors, x + 1)
                for t in range(FT):
                    nc.tensor.transpose(tr[:, 0, t * P:(t + 1) * P], feats[:, t * P:(t + 1) * P], ident[:, :])
                nc.tensor.transpose(tr[0:PART, 0, FT * P:(FT + 1) * P], feats[:, FT * P:PACKED],
                                    ident[:, :]).then_inc(f_trans, 1)

            x_dots = x_both[0:DIM, :, 0:CATE, :].rearrange("p h f (s j) -> p h (f s) j", s=4)

            def gram(x, q, first=False):
                if q >= 4 or not first:
                    pe.wait_ge(gram_taken, FILLS * x + q - 3)
                if q == 1:
                    pe.wait_ge(feat_done, x + 1)
                n = 4 * CATE
                for c in range(PER_FILL):
                    j = PER_FILL * q + c
                    bank = (gr, tr)[q // 2 % 2][0:n, q % 2, :]
                    last = nc.tensor.matmul(bank[:, c * 2 * n:(c + 1) * 2 * n], x_dots[:, 0, :, j],
                                            x_dots[:, :, :, j], start=True, stop=True)
                last.then_inc(gram_ready, 1)

            pe.wait_ge(ident_ready, 2)
            pe.wait_ge(e13_in, 32)
            nc.tensor.transpose(tr[:, 0, 0:CONT], e13[:, :, :].rearrange("p a d -> p (a d)"),
                                ident[0:CONT, 0:CONT]).then_inc(eT_ready, 1)
            pe.wait_ge(vbd_ready, 1)
            nc.tensor.matmul(tr[:, 1, 0:1], ee[:, 0:P], ones, start=True, stop=True)
            nc.tensor.matmul(tr[0:PART, 1, 1:2], ee[:, P:FAC], ones, start=True, stop=True).then_inc(s_ready, 1)
            for n in range(V_TILES):
                pe.wait_ge(v_rows_in[n], 16)
                rows_n = v_rows(n)
                for h in range(2):
                    last = nc.tensor.matmul(acc[1][0:CONT, h, :], vbd[0:rows_n.shape[0], n, :],
                                            rows_n[:, h * HALF:(h + 1) * HALF],
                                            start=n == 0, stop=n == V_TILES - 1)
            last.then_inc(v_done, 1)

            def early(kt, fills=()):
                pe.wait_ge(w1_split, kt + 1)
                for h in range(2):
                    half_k_tile(0, kt, h)
                    for q in fills[h * len(fills) // 2:(h + 1) * len(fills) // 2]:
                        gram(0, q, first=True)

            pe.wait_ge(setup_done, 1)
            for g in range(NG):
                transpose_group(0, g, first=True)
                for kt in USE_K[0][g]:
                    early(kt)
                cont_cate(0, g)
            factor(0)
            for kt in range(EK - 5, EK - 3):
                early(kt, range(FILLS)[(kt - EK + 5) * FILLS // 2:][:FILLS // 2])

            def iteration(x, par, first=False, last=False):
                if not isinstance(x, int) or x >= 2:
                    pe.wait_ge(norm_act, x - 1)
                    pe.wait_ge(norm_dve, x - 1)
                if first:
                    for g in range(NG):
                        transpose_group(x + 1, g)
                        for kt in USE_K[1][g]:
                            if kt == EK:
                                pe.wait_ge(f_lo, x + 1)
                            early(kt)
                        cont_cate(x + 1, g)
                    factor(x + 1)
                for kt in range(EK + 2 if first else 0, KT):
                    if first:
                        pe.wait_ge(w1_split, kt + 1)
                    if kt == EK:
                        pe.wait_ge(f_lo, x + 1)
                    if kt == EK + FT:
                        pe.wait_ge(late_done[0], x + 1)
                    if kt == EK + FT + 1:
                        pe.wait_ge(late_done[1], x + 1)
                    for h in range(2):
                        done = half_k_tile(par, kt, h)
                        if kt == EK + 1 and h == 0 and not last:
                            cont_cate(x + 1, NG - 1)
                            factor(x + 1)
                        if kt == EK + FT - 1 and h == 1 and not last:
                            done.then_inc(f_used, 1)
                        if kt >= EK + FT and not last:
                            q = 3 * (2 * (kt - EK - FT) + h)
                            for q in range(max(q - 2, 0), q + 1):
                                gram(x + 1, q)
                    if kt == KT - 1:
                        done.then_inc(acc_ready, 1)
                    elif last:
                        done.then_inc(w1_free, 1)
                    if last:
                        if kt == K2 - 1:
                            transpose2(0, 0)
                        if kt == EK + FT - 1:
                            product2(0, 0, first=True)
                        continue
                    for g, (a, b) in enumerate(GROUPS):
                        if kt == b - 1:
                            if g > 0:
                                cont_cate(x + 1, g - 1)
                            transpose_group(x + 1, g)

            def transpose2(x, par):
                t = tr if par == 0 else gr
                if isinstance(x, int) and x < 2:
                    pe.wait_ge(feat_done, TILES)
                    pe.wait_ge(gram_taken, FILLS * TILES)
                pe.wait_ge(h1_in[par], 8 * x + 16 - 8 * par)
                if not isinstance(x, int) or x >= 2:
                    pe.wait_ge(y_ready, K2 * (x - 1))
                for k in range(K2):
                    last = nc.tensor.transpose(t[:, k // 4, (k % 4) * P:(k % 4 + 1) * P],
                                               h1[par][:, k * P:(k + 1) * P], ident[:, :])
                last.then_inc(t2_ready, 1)

            def product2(x, par, first=False, last=False):
                if isinstance(x, int) and x in (0, 2):
                    pe.wait_ge(norm_act, TILES - 1 + x // 2)
                    pe.wait_ge(norm_dve, TILES - 1 + x // 2)
                elif isinstance(x, int) and x == 1:
                    pe.wait_ge(h2_done, 1)
                else:
                    pe.wait_ge(h2_done, x - 1)
                pe.wait_ge(y_split, x + 1)
                for k in range(K2):
                    if first:
                        pe.wait_ge(w2_done, k + 1)
                    for h in range(2):
                        done = three(sums2(x, par)[:, h, :], y_hi[:, par, k, :], y_lo[:, par, k, :],
                                     w2_hi[:, k, h * HALF:(h + 1) * HALF],
                                     w2_lo[:, k, h * HALF:(h + 1) * HALF], k == 0, k == K2 - 1)
                    if k == 0 and not last:
                        transpose2(x + 1, 1 - par)
                done.then_inc(acc2_ready, 1)

            iteration(0, 0, first=True)
            iteration(1, 1)
            iteration(2, 0)
            with pe.Fori(0, (TILES - 4) // 2) as i:
                for u in range(2):
                    iteration(2 * i + (3 + u), 1 - u)
            iteration(TILES - 1, 1, last=True)

            product2(1, 1)
            product2(2, 0)
            product2(3, 1)
            with pe.Fori(0, (TILES - 6) // 2) as i:
                for u in range(2):
                    product2(2 * i + (4 + u), u)
            product2(TILES - 2, 0)
            product2(TILES - 1, 1, last=True)

        @block.scalar
        def _(act):
            conts_v = conts.rearrange("(p x) f -> p x f", x=TILES)

            def load_conts(x, par, first=False):
                if not first:
                    act.wait_ge(factors, x - 1)
                    stands_alone(act)
                src = conts_v[:, at(x), :].rearrange("p o f -> p (o f)")
                for r in range(2):
                    act.dma_start(c2[:, par, r * CONT:(r + 1) * CONT], src).then_inc(conts_in[par], 16)

            cates_v = cates.rearrange("(p x) f -> p x f", x=TILES)

            def load_cates(x, par, first=False):
                if not first:
                    act.wait_ge(idx_step, 4 * x - 4)
                    stands_alone(act)
                act.dma_start(cates_sb[:, par, :],
                              cates_v[:, at(x), :].rearrange("p o f -> p (o f)")).then_inc(cates_in[par], 16)

            def h1_store(x):
                act.wait_ge(norm_act, x + 1)
                act.wait_ge(norm_dve, x + 1)
                stands_alone(act)
                act.dma_start(h1_dram[:, at(x), :].rearrange("p o n -> p (o n)"), h1_row[:, :]).then_inc(h1_out, 16)

            load_cates(0, 0, first=True)
            load_cates(1, 1, first=True)
            load_conts(0, 0, first=True)
            load_conts(1, 1, first=True)
            act.dma_start(rows_sb[:, :], rows.bitcast(U32)).then_inc(rows_in, 16)
            with nc.allow_non_contiguous_dma(reason="a parameter to each partition"):
                act.dma_start(g1_col[:, :], g1.rearrange("(n p) -> p n", p=P)).then_inc(g1_in, 16)
                act.dma_start(be1_col[:, :], be1.rearrange("(n p) -> p n", p=P)).then_inc(g1_in, 16)
            act.dma_start(bout_bc[:, :], bout.unsqueeze(0).to_broadcast([P, 1])).then_inc(g1_in, 16)
            load_cates(2, 0)
            load_cates(3, 1)

            def split_group(x, g):
                a, b = GROUPS[g]
                n = (b - a) * P
                act.wait_ge(trans_ready, NG * x + g + 1)
                nc.scalar.copy(x_hi[:, a:b, :].rearrange("p k b -> p (k b)"), tr[:, 0, 0:n]).then_inc(ts_hi, 1)
                act.wait_ge(ts_hi, 2 * NG * x + 2 * g + 1)
                nc.scalar.copy(x_hi[0:DIM, EK + a:EK + b, :], x_hi[DIM:P, a:b, :]).then_inc(ts_hi, 1)

            def factors_copy(x):
                act.wait_ge(f_trans, x + 1)
                nc.scalar.copy(feats[:, 0:FT * P], tr[:, 0, 0:FT * P])
                nc.scalar.copy(cc_dots[:, 0:2 * P].rearrange("p (t b) -> p t b", t=2),
                               tr[:, 1, :].rearrange("p (t h b) -> p h t b", t=2, h=2)[:, 1])
                nc.scalar.activation(cc_dots[:, 2 * P:3 * P], gr[:, 1, P:2 * P], ACT.Identity, bias=fac[:, 0:1])
                if not isinstance(x, int) or x >= 1:
                    act.wait_ge(late_done[0], x)
                nc.scalar.activation(late[0:PART, 0, :], tr[0:PART, 0, FT * P:], ACT.Identity,
                                     scale=fac[0:PART, 1:2]).then_inc(factors_t, 1)

            def take_dots(x, q, first=False):
                act.wait_ge(gram_ready, FILLS * x + q + 1)
                if q == 0 and not first:
                    act.wait_ge(dots_out, 128 * x)
                to = dots[:, :, :, PER_FILL * q:PER_FILL * (q + 1)]
                nc.scalar.mul(to, gram_part(q, 0), 0.5).then_inc(gram_half, 1)

            def features(x, first=False):
                act.wait_ge(feat_done, x + 1)
                if not first:
                    act.wait_ge(f_used, x)
                nc.scalar.copy(x_hi[:, F_ROW:F_ROW + FT, :].rearrange("p k b -> p (k b)"),
                               feats[:, 0:FT * P]).then_inc(f_hi, 1)

            def root(x):
                act.wait_ge(ln, LN_STEPS * x + 3)
                nc.scalar.activation(st[:, 1:2], st[:, 0:1], ACT.Sqrt).then_inc(sqrt_done, 1)

            def norm1(x, par):
                root(x)
                act.wait_ge(ln, LN_STEPS * x + 8)
                if not isinstance(x, int) or x >= 1:
                    act.wait_ge(h1_out, 16 * x)
                nc.scalar.activation(h1_row[:, 0:HALF], acc[par][:, 0, :], ACT.Identity,
                                     bias=st[:, 7:8], scale=st[:, 6:7]).then_inc(norm_act, 1)

            def w1_hi_part(k):
                act.wait_ge(w1_in[k], 16)
                if k == EK:
                    act.wait_ge(v_done, 1)
                if k == EK + FT:
                    act.wait_ge(b1_in, 16)
                    nc.scalar.copy(raw_lo[k][V_AT:V_AT + CONT, :],
                                   acc[1][0:CONT, :, :].rearrange("p h n -> p (h n)")).then_inc(v_in, 1)
                    act.wait_ge(v_in, 1)
                m = rows_of(k)
                nc.scalar.copy(w1_hi[0:m, k, :], raw_lo[k][0:m, :]).then_inc(w1_rounded, 1)

            for g, ks in enumerate(SPLIT_K[0]):
                for k in ks:
                    w1_hi_part(k)
                split_group(0, g)
            factors_copy(0)
            for q in range(FILLS):
                take_dots(0, q, first=True)
            features(0, first=True)

            def iteration(x, par, first=False):
                if not first:
                    norm1(x - 1, 1 - par)
                for g in range(NG):
                    for k in SPLIT_K[1][g] if first else ():
                        w1_hi_part(k)
                    split_group(x + 1, g)
                    if g == 0 and not first:
                        h1_store(x - 1)
                    if g == 1 and (not isinstance(x, int) or x < TILES - 2):
                        load_conts(x + 2, par)
                    if g == 1 and (not isinstance(x, int) or 0 < x < TILES - 3):
                        load_cates(x + 3, 1 - par)
                factors_copy(x + 1)
                for q in range(FILLS):
                    take_dots(x + 1, q)
                features(x + 1)

            iteration(0, 0, first=True)
            iteration(1, 1)
            iteration(2, 0)
            with act.Fori(0, (TILES - 6) // 2) as i:
                for u in range(2):
                    iteration(2 * i + (3 + u), 1 - u)
            iteration(TILES - 3, 1)
            iteration(TILES - 2, 0)
            norm1(TILES - 2, 0)
            h1_store(TILES - 2)

            def relu1(x, par):
                t = tr if par == 0 else gr
                act.wait_ge(t2_ready, x + 1)
                if not isinstance(x, int) or x >= 1:
                    act.wait_ge(y_split, x)
                for k in range(K2):
                    nc.scalar.activation(y[:, k, :], t[:, k // 4, (k % 4) * P:(k % 4 + 1) * P], ACT.Relu,
                                         bias=be1_col[:, k:k + 1], scale=g1_col[:, k:k + 1]).then_inc(y_ready, 1)

            def norm2(x, par):
                root(x + TILES)
                act.wait_ge(ln, LN_STEPS * x + (LN_STEPS * TILES + 8))
                if not isinstance(x, int) or x >= 2:
                    act.wait_ge(a2_mul, x - 1)
                nc.scalar.activation(n2[par][:, :], h2, ACT.Identity,
                                     bias=st[:, 7:8], scale=st[:, 6:7]).then_inc(n2_ready, 1)

            act.wait_ge(w1_free, 4)
            act.wait_ge(h1_out, 16 * 2)
            load_h1(act, 0, 0)
            load_h1(act, 1, 1)
            act.wait_ge(g1_in, 48)
            for k in range(K2 + 2):
                if k < K2:
                    act.wait_ge(w1_free, W2_AT + k + 1)
                    act.dma_start(raw_lo[W2_AT + k][:, :], W2[k * P:k * P + P, :]).then_inc(w2_in[k], 16)
                if k == 2:
                    relu1(0, 0)
                if k >= 2:
                    act.wait_ge(w2_in[k - 2], 16)
                    nc.scalar.copy(w2_hi[:, k - 2, :], raw_lo[W2_AT + k - 2][:, :]).then_inc(w2_hi_done, 1)
            relu1(1, 1)
            relu1(2, 0)
            norm1(TILES - 1, 1)
            h1_store(TILES - 1)
            act.wait_ge(acc_ready, TILES)
            norm2(0, 0)
            norm2(1, 1)
            relu1(3, 1)
            norm2(2, 0)
            relu1(4, 0)
            with act.Fori(0, (TILES - 6) // 2) as i:
                for u in range(2):
                    norm2(2 * i + (3 + u), 1 - u)
                    relu1(2 * i + (5 + u), 1 - u)
            norm2(TILES - 3, 1)
            relu1(TILES - 1, 1)
            norm2(TILES - 2, 0)
            root(TILES - 1 + TILES)
            act.wait_ge(logit_done, TILES)
            nc.scalar.activation(prob[:, :], logit[:, :], ACT.Sigmoid, bias=bout_bc[:, 0:1]).then_inc(prob_done, 1)

        @block.vector
        def _(dve):
            TT = nc.vector.tensor_tensor
            TS = nc.vector.tensor_scalar
            STT = nc.vector.scalar_tensor_tensor
            done = [0]

            def step(ins):
                done[0] += 1
                ins.then_inc(setup, 1)

            def indices(x, par):
                dve.wait_ge(cates_in[par], 8 * x + 16 - 8 * par)
                nc.vector.tensor_copy(cates_f[:, :], cates_sb[:, par, :]).then_inc(idx_step, 1)
                dve.wait_ge(idx_step, 4 * x + 1)
                TS(shift[:, :], cates_f[:, :], 0.0, float(VOCAB), ALU.is_lt, ALU.mult).then_inc(idx_step, 1)
                dve.wait_ge(idx_step, 4 * x + 2)
                TT(cates_f[:, :], cates_f[:, :], shift[:, :], ALU.add).then_inc(idx_step, 1)
                dve.wait_ge(idx_step, 4 * x + 3)
                TS(idx[:, par, :].bitcast(I32), cates_f[:, :], 0.0, float(VOCAB - 1),
                   ALU.max, ALU.min).then_inc(idx_step, 1)

            win = feats[:, 0:WIN]
            step(nc.vector.memset(win, 0.0))
            step(nc.vector.memset(vbd[:, :, :], 0.0))
            step(nc.vector.memset(ee, 0.0))
            step(nc.vector.memset(feats[:, PACKED - 1:PACKED], 1.0))
            nc.vector.memset(late_t[:, :, :], 0.0)
            indices(0, 0)
            dve.wait_ge(eT_ready, 1)
            step(nc.vector.tensor_copy(eT[:, :], tr[:, 0, 0:CONT]))
            dve.wait_ge(setup, done[0])
            vflat = vbd[:, :, :].rearrange("p n i -> p (n i)")
            hop = CONT + 2
            nc.vector.tensor_copy(vflat[0:DIM, 0::hop], eT[0:DIM, 0::2])
            nc.vector.tensor_copy(vflat[DIM:P, 1::hop], eT[DIM:P, 1::2])
            for k in range(1, CONT // 2 + 1):
                o = FAC_AT + (k - 1) * CONT
                TT(ee[:, o:o + CONT - k], eT[0:DIM, 0:CONT - k], eT[0:DIM, k:CONT], ALU.mult)
                TT(ee[:, o + CONT - k:o + CONT], eT[0:DIM, CONT - k:CONT], eT[0:DIM, 0:k], ALU.mult)
            nc.vector.memset(ee[0:1, FAC_AT + NN:FAC], 1.0).then_inc(vbd_ready, 1)
            nc.vector.tensor_copy(win[0:DIM, P:P + CONT], eT[0:DIM, :])
            step(nc.vector.tensor_copy(win[DIM:P, P + CONT:P + 2 * CONT], eT[DIM:P, :]))
            dve.wait_ge(setup, done[0])
            step(nc.vector.tensor_copy(win_hi[:, :], win))
            dve.wait_ge(setup, done[0])
            step(TT(win_lo[:, :], win, win_hi[:, :].bitcast(F32), ALU.subtract))
            dve.wait_ge(setup, done[0])
            dve.wait_ge(s_ready, 1)
            nc.vector.tensor_copy(fac[:, 0:1], tr[:, 1, 0:1])
            nc.vector.tensor_copy(fac[0:PART, 1:2], tr[0:PART, 1, 1:2]).then_inc(setup_done, 1)

            def split_group(x, g):
                a, b = GROUPS[g]
                n = (b - a) * P
                dve.wait_ge(ts_hi, 2 * NG * x + 2 * g + 1)
                TT(x_lo[:, a:b, :].rearrange("p k b -> p (k b)"), tr[:, 0, 0:n],
                   x_hi[:, a:b, :].rearrange("p k b -> p (k b)").bitcast(F32), ALU.subtract)
                dve.wait_ge(ts_hi, 2 * NG * x + 2 * g + 2)
                TT(x_lo[0:DIM, EK + a:EK + b, :].rearrange("p k b -> p (k b)"), tr[DIM:P, 0, 0:n],
                   x_hi[DIM:P, a:b, :].rearrange("p k b -> p (k b)").bitcast(F32),
                   ALU.subtract).then_inc(ts_lo, 1)

            def w1_lo_part(k):
                m = rows_of(k)
                dve.wait_ge(w1_rounded, k + 1)
                TT(w1_lo[0:m, k, :], raw_lo[k][0:m, :], w1_hi[0:m, k, :].bitcast(F32),
                   ALU.subtract).then_inc(w1_split, 1)

            def packed_factors(x, par):
                dve.wait_ge(conts_in[par], 16 * x + 32 - 16 * par)
                if not isinstance(x, int) or x >= 1:
                    dve.wait_ge(f_lo, x)
                nc.vector.tensor_copy(feats[:, 0:CC].rearrange("p (g i) -> p g i", i=CONT),
                                      c2[:, par, 0:CONT].unsqueeze(1).to_broadcast([P, CATE, CONT]))
                nc.vector.tensor_copy(feats[:, CC + NN:PACKED - 1], c2[:, par, 0:CONT])
                for k in range(1, CONT // 2 + 1):
                    last = TT(feats[:, CC + (k - 1) * CONT:CC + k * CONT], c2[:, par, 0:CONT],
                              c2[:, par, k:k + CONT], ALU.mult)
                last.then_inc(factors, 1)

            def packed_features(x):
                dve.wait_ge(factors_t, x + 1)
                TT(cc_dots[:, 0:2 * P].rearrange("p (t b) -> p t b", t=2),
                   tr[:, 1, :].rearrange("p (t h b) -> p h t b", t=2, h=2)[:, 0],
                   cc_dots[:, 0:2 * P].rearrange("p (t b) -> p t b", t=2), ALU.add)
                TT(cc_dots[:, 2 * P:3 * P], gr[:, 1, 0:P], cc_dots[:, 2 * P:3 * P], ALU.add).then_inc(cc_sum, 1)
                dve.wait_ge(cc_sum, x + 1)
                TT(feats[:, 0:FT * P], cc_dots[:, :], feats[:, 0:FT * P], ALU.mult).then_inc(feat_done, 1)

            def take_dots(x, q):
                dve.wait_ge(gram_half, FILLS * x + q + 1)
                to = dots[:, :, :, PER_FILL * q:PER_FILL * (q + 1)]
                TT(to, gram_part(q, 1), to, ALU.add).then_inc(gram_taken, 1)

            def features_lo(x):
                dve.wait_ge(f_hi, x + 1)
                TT(x_lo[:, F_ROW:F_ROW + FT, :].rearrange("p k b -> p (k b)"), feats[:, 0:FT * P],
                   x_hi[:, F_ROW:F_ROW + FT, :].rearrange("p k b -> p (k b)").bitcast(F32),
                   ALU.subtract).then_inc(f_lo, 1)

            def late_features(x, n):
                dve.wait_ge(late_in[n], LATE_IN[n] * x + LATE_IN[n])
                if n == 0:
                    dve.wait_ge(feat_done, x + 1)
                m, a, b = (SHARED, 0, 1) if n == 0 else (WHOLE, 1, 3)
                hi, lo = [t[0:m, F_ROW + FT + a:F_ROW + FT + b, :] for t in (x_hi, x_lo)]
                TT(late[0:m, a:b, :], late[0:m, a:b, :], late_t[0:m, a:b, :], ALU.add).then_inc(late_sum[n], 1)
                dve.wait_ge(late_sum[n], x + 1)
                nc.vector.tensor_copy(hi, late[0:m, a:b, :]).then_inc(late_hi[n], 1)
                dve.wait_ge(late_hi[n], x + 1)
                TT(lo, late[0:m, a:b, :], hi.bitcast(F32), ALU.subtract).then_inc(late_done[n], 1)

            def layer_norm(x, rows, used):
                b = LN_STEPS * x
                for h in range(2):
                    last = nc.vector.bn_stats(bn[:, h, :], rows[:, h, :])
                last.then_inc(ln, 1)
                dve.wait_ge(ln, b + 1)
                stands_alone(dve)
                nc.vector.bn_aggr(mv[:, :], bn[:, :, :].rearrange("p h s -> p (h s)")).then_inc(ln, 1)
                dve.wait_ge(ln, b + 2)
                TS(st[:, 0:1], mv[:, 1:2], EPS, None, ALU.add).then_inc(ln, 1)
                dve.wait_ge(sqrt_done, x + 1)
                nc.vector.reciprocal(st[:, 2:3], st[:, 1:2]).then_inc(ln, 1)
                dve.wait_ge(ln, b + 4)
                STT(st[:, 3:4], st[:, 2:3], st[:, 2:3], st[:, 0:1], ALU.mult, ALU.mult).then_inc(ln, 1)
                dve.wait_ge(ln, b + 5)
                TS(st[:, 4:5], st[:, 3:4], -0.5, 1.5, ALU.mult, ALU.add).then_inc(ln, 1)
                dve.wait_ge(ln, b + 6)
                if used is not None:
                    dve.wait_ge(*used)
                TT(st[:, 6:7], st[:, 2:3], st[:, 4:5], ALU.mult).then_inc(ln, 1)
                dve.wait_ge(ln, b + 7)
                STT(st[:, 7:8], mv[:, 0:1], -1.0, st[:, 6:7], ALU.mult, ALU.mult).then_inc(ln, 1)

            def norm1(x, par):
                dve.wait_ge(acc_ready, x + 1)
                first = isinstance(x, int) and x == 0
                layer_norm(x, acc[par], None if first else (norm_act, x))
                if not first:
                    dve.wait_ge(h1_out, 16 * x)
                TS(h1_row[:, HALF:HID], acc[par][:, 1, :], mv[:, 0:1], st[:, 6:7],
                   ALU.subtract, ALU.mult).then_inc(norm_dve, 1)

            indices(1, 1)
            packed_factors(0, 0)
            for g, ks in enumerate(SPLIT_K[0]):
                for k in ks:
                    w1_lo_part(k)
                split_group(0, g)
            packed_features(0)
            for q in range(FILLS):
                take_dots(0, q)
            features_lo(0)

            def iteration(x, par, first=False):
                if not isinstance(x, int) or x < TILES - 2:
                    indices(x + 2, par)
                if not first:
                    norm1(x - 1, 1 - par)
                packed_factors(x + 1, 1 - par)
                for g in range(NG):
                    for k in SPLIT_K[1][g] if first else ():
                        w1_lo_part(k)
                    split_group(x + 1, g)
                late_features(x, 0)
                if first:
                    late_features(x, 1)
                packed_features(x + 1)
                if not first:
                    late_features(x, 1)
                for q in range(FILLS):
                    take_dots(x + 1, q)
                features_lo(x + 1)

            iteration(0, 0, first=True)
            iteration(1, 1)
            iteration(2, 0)
            with dve.Fori(0, (TILES - 6) // 2) as i:
                for u in range(2):
                    iteration(2 * i + (3 + u), 1 - u)
            iteration(TILES - 3, 1)
            iteration(TILES - 2, 0)
            norm1(TILES - 2, 0)

            def split_y(x, par):
                dve.wait_ge(y_ready, K2 * x + K2)
                if not isinstance(x, int) or x >= 2:
                    dve.wait_ge(acc2_ready, x - 1)
                nc.vector.tensor_copy(y_hi[:, par, :, :], y[:, :, :]).then_inc(y_hi_done, 1)
                dve.wait_ge(y_hi_done, x + 1)
                TT(y_lo[:, par, :, :], y[:, :, :], y_hi[:, par, :, :].bitcast(F32), ALU.subtract).then_inc(y_split, 1)

            def add_b2(x, par):
                dve.wait_ge(acc2_ready, x + 1)
                if not isinstance(x, int) or x >= 1:
                    dve.wait_ge(n2_ready, x)
                TT(h2.rearrange("p (h n) -> p h n", h=2), sums2(x, par)[:, :, :],
                   b2_bc.rearrange("p (h n) -> p h n", h=2), ALU.add).then_inc(h2_done, 1)

            def norm2(x, par):
                if not isinstance(x, int) or x >= 1:
                    add_b2(x, par)
                dve.wait_ge(h2_done, x + 1)
                layer_norm(x + TILES, h2.rearrange("p (h n) -> p h n", h=2), None)

            def affine2_whole(x, par):
                dve.wait_ge(a2_ready, x)
                STT(a2[par][:, :], h2, mv[:, 0:1], g2_bc, ALU.subtract, ALU.mult).then_inc(a2_mul, 1)
                dve.wait_ge(a2_mul, x + 1)
                STT(a2[par][:, :], a2[par][:, :], st[:, 6:7], be2_bc, ALU.mult, ALU.add).then_inc(a2_ready, 1)

            def product_out(x, par):
                dve.wait_ge(a2_ready, x + 1)
                if not isinstance(x, int) or x >= 1:
                    dve.wait_ge(logit_done, x)
                STT(r2, a2[par][:, :], 0.0, wout_bc, ALU.max, ALU.mult,
                    accum_out=logit[:, at(x)]).then_inc(logit_done, 1)

            split_y(0, 0)
            for k in range(K2):
                dve.wait_ge(w2_hi_done, k + 1)
                TT(w2_lo[:, k, :], raw_lo[W2_AT + k][:, :], w2_hi[:, k, :].bitcast(F32),
                   ALU.subtract).then_inc(w2_done, 1)
            for n in range(2):
                late_features(TILES - 1, n)
            split_y(1, 1)
            dve.wait_ge(par_in, 16 * 4)
            add_b2(0, 0)
            norm1(TILES - 1, 1)
            dve.wait_ge(acc_ready, TILES)
            split_y(2, 0)
            norm2(0, 0)
            norm2(1, 1)
            split_y(3, 1)
            product_out(0, 0)
            norm2(2, 0)
            split_y(4, 0)
            product_out(1, 1)
            with dve.Fori(0, (TILES - 6) // 2) as i:
                for u in range(2):
                    norm2(2 * i + (3 + u), 1 - u)
                    split_y(2 * i + (5 + u), 1 - u)
                    product_out(2 * i + (2 + u), u)
            norm2(TILES - 3, 1)
            split_y(TILES - 1, 1)
            product_out(TILES - 4, 0)
            norm2(TILES - 2, 0)
            product_out(TILES - 3, 1)
            norm2(TILES - 1, 1)
            product_out(TILES - 2, 0)
            affine2_whole(TILES - 1, 1)
            product_out(TILES - 1, 1)


_INS = ["r_conts", "r_cates", "L0_rec_emb_table", "L0_rec_W1", "L0_rec_b1", "L0_rec_ln1_g", "L0_rec_ln1_b",
        "L0_rec_W2", "L0_rec_b2", "L0_rec_ln2_g", "L0_rec_ln2_b", "L0_rec_Wout", "L0_rec_bout"]


def kernel(**inputs):
    import concourse.bacc as bacc
    from concourse.bass_utils import run_bass_kernel_spmd

    nc = bacc.Bacc("TRN2", target_bir_lowering=False, num_devices=1, dynamic_dma_scratch_size=2048)
    arrays, args = {}, []
    for name in _INS:
        a = np.ascontiguousarray(inputs[name])
        arrays[f"in_{name}"] = a
        args.append(nc.dram_tensor(f"in_{name}", a.shape, mybir.dt.from_np(a.dtype), kind="ExternalInput").ap())
    arrays["feature_rows"] = feature_rows()
    args.append(nc.dram_tensor("feature_rows", (P, FK), I32, kind="ExternalInput").ap())
    args.append(nc.dram_tensor("out", (BATCH, 1), F32, kind="ExternalOutput").ap())
    build(nc, *args)
    r = run_bass_kernel_spmd(nc, [arrays], core_ids=[0])
    return r.results[0]["out"]
```
